# Optimizing a Trainium2 kernel written in Bass

```python
import numpy as np
import jax
import jax.numpy as jnp

def _softmax(x, axis=-1):
    return jax.nn.softmax(x, axis=axis)

def _gelu(x):
    return jax.nn.gelu(x, approximate=True)

def _silu(x):
    return jax.nn.silu(x)

def _sigmoid(x):
    return jax.nn.sigmoid(x)

def _layernorm(x, axis=-1, eps=1e-05):
    m = jnp.mean(x, axis=axis, keepdims=True)
    v = jnp.var(x, axis=axis, keepdims=True)
    return (x - m) / jnp.sqrt(v + eps)

def _scatter_add(tgt, idx, src, axis=0):
    return tgt.at[idx].add(src)

def _segment_sum(src, seg, n):
    return jax.ops.segment_sum(src, seg, n)
kernel_name = 'mk_xattn_ffn_d2_seqx_r8_071260'

def setup_inputs(seed: int=0):
    np.random.seed(seed)
    _w = jnp.asarray

    def _rec_inputs():
        import jax
        import jax.numpy as jnp
        _rk = jax.random.key(seed)
        x = -0.0003929 + 0.9999 * jax.random.normal(jax.random.fold_in(_rk, 1), (4, 256, 512), jnp.float32)
        _lenS = 256 - jax.random.randint(jax.random.fold_in(_rk, 7), (4,), 0, max(1, 256 // 4) + 1, jnp.int32)
        _lenS2 = 1601 - jax.random.randint(jax.random.fold_in(_rk, 8), (4,), 0, max(1, 1601 // 4) + 1, jnp.int32)
        _ctx_4096P = jax.random.normal(jax.random.fold_in(_rk, 11), (4, 16, 512), jnp.float32)
        _ctx_4096c = jax.random.dirichlet(jax.random.fold_in(_rk, 511), 0.3 * jnp.ones((16,), jnp.float32), (4, 1601))
        _ctx_4096t = jnp.einsum('bsk,bkd->bsd', _ctx_4096c, _ctx_4096P)
        _ctx_4096t = _ctx_4096t * jax.lax.rsqrt(jnp.mean(jnp.square(_ctx_4096t)) + 1e-12) * 0.953939
        ctx_4096 = 2.81802e-05 + 1.00001 * (_ctx_4096t + 0.3 * jax.random.normal(jax.random.fold_in(_rk, 611), (4, 1601, 512), jnp.float32))
        _validS = jnp.arange(256)[None, :] < _lenS[:, None]
        _validS2 = jnp.arange(1601)[None, :] < _lenS2[:, None]
        _causal = jnp.tril(jnp.ones((256, 256), dtype=bool))
        mask_1x1xSxS2_ff0 = jnp.where(jnp.ones((1, 1, 256, 1601), dtype=bool), 0.0, -1000000000.0).astype(jnp.float32)
        return (x, ctx_4096, mask_1x1xSxS2_ff0)
    x, ctx_4096, mask_1x1xSxS2_ff0 = _rec_inputs()

    def _L0_xattn_setup():
        import jax, jax.numpy as jnp
        import numpy as np
        B, N, NKV = (2, 256, 256)
        E = 512
        H = 16
        HD = E // H
        LQ = E // 8
        LKV = E // 16
        key = jax.random.key(seed)
        ks = jax.random.split(key, 6)
        Q = jax.random.normal(ks[0], (B, N, E), dtype=jnp.float32)
        K = jax.random.normal(ks[1], (B, NKV, E), dtype=jnp.float32)
        Wq_d = jax.random.normal(ks[2], (E, LQ), dtype=jnp.float32) / np.sqrt(E)
        W_qk = jax.random.normal(ks[3], (LQ, H * LKV), dtype=jnp.float32) / np.sqrt(LQ)
        Wkv_d = jax.random.normal(ks[4], (E, LKV), dtype=jnp.float32) / np.sqrt(E)
        Wv_u = jax.random.normal(ks[5], (LKV, H * HD), dtype=jnp.float32) / np.sqrt(LKV)
        return {'Q': Q, 'K': K, 'Wq_d': Wq_d, 'W_qk': W_qk, 'Wkv_d': Wkv_d, 'Wv_u': Wv_u}
    _L0_xattn_all = _L0_xattn_setup()
    _L0_xattn_in = {k: v for k, v in _L0_xattn_all.items() if k in ('Wq_d', 'W_qk', 'Wkv_d', 'Wv_u')}
    del _L0_xattn_all

    def _L0_ffn_setup():
        import jax, jax.numpy as jnp
        import numpy as np
        B, S, D_IN, D_OUT = (2, 256, 512, 512)
        E, K, R = (8, 2, 16)
        SCALING = 32.0 / 16.0
        key = jax.random.key(seed)
        ks = jax.random.split(key, 6)
        x = jax.random.normal(ks[0], (B, S, D_IN), dtype=jnp.float32)
        gate_w = jax.random.normal(ks[1], (E, D_IN), dtype=jnp.float32) * 0.02
        base_w = jax.random.normal(ks[2], (D_OUT, D_IN), dtype=jnp.float32) * 0.02
        base_b = jax.random.normal(ks[3], (D_OUT,), dtype=jnp.float32) * 0.02
        lora_A = jax.random.normal(ks[4], (E, R, D_IN), dtype=jnp.float32) * 0.02
        lora_B = jax.random.normal(ks[5], (E, D_OUT, R), dtype=jnp.float32) * 0.02
        return {'x': x, 'gate_w': gate_w, 'base_w': base_w, 'base_b': base_b, 'lora_A': lora_A, 'lora_B': lora_B}
    _L0_ffn_all = _L0_ffn_setup()
    _L0_ffn_in = {k: v for k, v in _L0_ffn_all.items() if k in ('gate_w', 'base_w', 'base_b', 'lora_A', 'lora_B')}
    del _L0_ffn_all

    def _L1_xattn_setup():
        import jax, jax.numpy as jnp
        import numpy as np
        B, Q, K, D = (1, 128, 6404, 512)
        H, KVH, HD = (32, 8, 128)
        GROUPS = H // KVH
        EPS = 1e-05

        def _rmsnorm(x, w):
            xf = x.astype(jnp.float32)
            var = jnp.mean(xf * xf, axis=-1, keepdims=True)
            return (xf * jax.lax.rsqrt(var + EPS)).astype(x.dtype) * w
        key = jax.random.key(seed)
        ks = jax.random.split(key, 8)
        s = 0.02
        return {'hidden_states': jax.random.normal(ks[0], (B, Q, D), jnp.float32), 'cross_attention_states': jax.random.normal(ks[1], (B, K, D), jnp.float32), 'attention_mask': jnp.zeros((B, 1, Q, K), jnp.float32), 'Wq': jax.random.normal(ks[2], (H * HD, D), jnp.float32) * s, 'Wk': jax.random.normal(ks[3], (KVH * HD, D), jnp.float32) * s, 'Wv': jax.random.normal(ks[4], (KVH * HD, D), jnp.float32) * s, 'Wo': jax.random.normal(ks[5], (D, H * HD), jnp.float32) * s, 'q_norm_w': jnp.ones((HD,), jnp.float32), 'k_norm_w': jnp.ones((HD,), jnp.float32)}
    _L1_xattn_all = _L1_xattn_setup()
    _L1_xattn_in = {k: v for k, v in _L1_xattn_all.items() if k in ('Wq', 'Wk', 'Wv', 'Wo', 'q_norm_w', 'k_norm_w')}
    del _L1_xattn_all

    def _L1_ffn_setup():
        import jax, jax.numpy as jnp
        import numpy as np
        H = 512
        I = 256
        E = 16
        TOPK = 4
        SI = 256
        key = jax.random.key(seed)
        ks = jax.random.split(key, 9)
        s = 0.02
        return {'hidden_states': jax.random.normal(ks[0], (2, 256, H), dtype=jnp.float32), 'gate_w': jax.random.normal(ks[1], (E, H), dtype=jnp.float32) * s, 'bias': jnp.zeros((E,), dtype=jnp.float32), 'Wg': jax.random.normal(ks[2], (E, I, H), dtype=jnp.float32) * s, 'Wu': jax.random.normal(ks[3], (E, I, H), dtype=jnp.float32) * s, 'Wd': jax.random.normal(ks[4], (E, H, I), dtype=jnp.float32) * s, 'Sg': jax.random.normal(ks[5], (SI, H), dtype=jnp.float32) * s, 'Su': jax.random.normal(ks[6], (SI, H), dtype=jnp.float32) * s, 'Sd': jax.random.normal(ks[7], (H, SI), dtype=jnp.float32) * s}
    _L1_ffn_all = _L1_ffn_setup()
    _L1_ffn_in = {k: v for k, v in _L1_ffn_all.items() if k in ('gate_w', 'bias', 'Wg', 'Wu', 'Wd', 'Sg', 'Su', 'Sd')}
    del _L1_ffn_all
    return {'x': x, 'ctx_4096': ctx_4096, 'mask_1x1xSxS2_ff0': mask_1x1xSxS2_ff0, 'L0_xattn_Wq_d': _L0_xattn_in['Wq_d'], 'L0_xattn_W_qk': _L0_xattn_in['W_qk'], 'L0_xattn_Wkv_d': _L0_xattn_in['Wkv_d'], 'L0_xattn_Wv_u': _L0_xattn_in['Wv_u'], 'L0_ffn_gate_w': _L0_ffn_in['gate_w'], 'L0_ffn_base_w': _L0_ffn_in['base_w'], 'L0_ffn_base_b': _L0_ffn_in['base_b'], 'L0_ffn_lora_A': _L0_ffn_in['lora_A'], 'L0_ffn_lora_B': _L0_ffn_in['lora_B'], 'L1_xattn_Wq': _L1_xattn_in['Wq'], 'L1_xattn_Wk': _L1_xattn_in['Wk'], 'L1_xattn_Wv': _L1_xattn_in['Wv'], 'L1_xattn_Wo': _L1_xattn_in['Wo'], 'L1_xattn_q_norm_w': _L1_xattn_in['q_norm_w'], 'L1_xattn_k_norm_w': _L1_xattn_in['k_norm_w'], 'L1_ffn_gate_w': _L1_ffn_in['gate_w'], 'L1_ffn_bias': _L1_ffn_in['bias'], 'L1_ffn_Wg': _L1_ffn_in['Wg'], 'L1_ffn_Wu': _L1_ffn_in['Wu'], 'L1_ffn_Wd': _L1_ffn_in['Wd'], 'L1_ffn_Sg': _L1_ffn_in['Sg'], 'L1_ffn_Su': _L1_ffn_in['Su'], 'L1_ffn_Sd': _L1_ffn_in['Sd']}

def reference(x, ctx_4096, mask_1x1xSxS2_ff0, L0_xattn_Wq_d, L0_xattn_W_qk, L0_xattn_Wkv_d, L0_xattn_Wv_u, L0_ffn_gate_w, L0_ffn_base_w, L0_ffn_base_b, L0_ffn_lora_A, L0_ffn_lora_B, L1_xattn_Wq, L1_xattn_Wk, L1_xattn_Wv, L1_xattn_Wo, L1_xattn_q_norm_w, L1_xattn_k_norm_w, L1_ffn_gate_w, L1_ffn_bias, L1_ffn_Wg, L1_ffn_Wu, L1_ffn_Wd, L1_ffn_Sg, L1_ffn_Su, L1_ffn_Sd):
    import jax
    import jax.numpy as jnp

    def _L0_xattn_ref(Q, K, Wq_d, W_qk, Wkv_d, Wv_u):
        import jax, jax.numpy as jnp
        import numpy as np
        B, N, NKV = (2, 256, 256)
        E = 512
        H = 16
        HD = E // H
        LQ = E // 8
        LKV = E // 16
        b, n, _ = Q.shape
        nkv = K.shape[1]
        C_q = Q @ Wq_d
        C_kv = K @ Wkv_d
        CqWqk = (C_q @ W_qk).reshape(b, n, H, LKV)
        scores = jnp.einsum('bnhl,bkl->bhnk', CqWqk, C_kv) / jnp.sqrt(jnp.asarray(LKV, dtype=Q.dtype))
        attn = jax.nn.softmax(scores, axis=-1)
        V_up = (C_kv @ Wv_u).reshape(b, nkv, H, HD)
        out = jnp.einsum('bhnk,bkhd->bnhd', attn, V_up)
        return out.reshape(b, n, H * HD)

    def _L0_ffn_ref(x, gate_w, base_w, base_b, lora_A, lora_B):
        import jax, jax.numpy as jnp
        import numpy as np
        B, S, D_IN, D_OUT = (2, 256, 512, 512)
        E, K, R = (8, 2, 16)
        SCALING = 32.0 / 16.0
        gate_logits = jnp.einsum('bsd,ed->bse', x, gate_w)
        weights, selected = jax.lax.top_k(gate_logits, K)
        weights = jax.nn.softmax(weights.astype(jnp.float32), axis=2).astype(x.dtype)
        result = jnp.einsum('bsd,od->bso', x, base_w) + base_b
        w_full = jnp.sum(jax.nn.one_hot(selected, E, dtype=x.dtype) * weights[..., None], axis=2)
        low = jnp.einsum('bsd,erd->ebsr', x, lora_A)
        lora_out = jnp.einsum('ebsr,eor,bse->bso', low, lora_B, w_full)
        result = result + SCALING * lora_out
        return result

    def _L1_xattn_ref(hidden_states, cross_attention_states, attention_mask, Wq, Wk, Wv, Wo, q_norm_w, k_norm_w):
        import jax, jax.numpy as jnp
        import numpy as np
        B, Q, K, D = (1, 128, 6404, 512)
        H, KVH, HD = (32, 8, 128)
        GROUPS = H // KVH
        EPS = 1e-05

        def _rmsnorm(x, w):
            xf = x.astype(jnp.float32)
            var = jnp.mean(xf * xf, axis=-1, keepdims=True)
            return (xf * jax.lax.rsqrt(var + EPS)).astype(x.dtype) * w
        bsz, q_len, _ = hidden_states.shape
        kv_len = cross_attention_states.shape[1]
        q = (hidden_states @ Wq.T).reshape(bsz, q_len, H, HD).transpose(0, 2, 1, 3)
        k = (cross_attention_states @ Wk.T).reshape(bsz, kv_len, KVH, HD).transpose(0, 2, 1, 3)
        v = (cross_attention_states @ Wv.T).reshape(bsz, kv_len, KVH, HD).transpose(0, 2, 1, 3)
        q = _rmsnorm(q, q_norm_w)
        k = jnp.repeat(k, GROUPS, axis=1)
        v = jnp.repeat(v, GROUPS, axis=1)
        k = _rmsnorm(k, k_norm_w)
        scale = 1.0 / np.sqrt(HD)
        scores = jnp.einsum('bhqd,bhkd->bhqk', q, k) * scale
        scores = scores + attention_mask[:, :, :, :kv_len]
        probs = jax.nn.softmax(scores.astype(jnp.float32), axis=-1).astype(q.dtype)
        out = jnp.einsum('bhqk,bhkd->bhqd', probs, v)
        out = out.transpose(0, 2, 1, 3).reshape(bsz, q_len, H * HD)
        return out @ Wo.T

    def _L1_ffn_ref(hidden_states, gate_w, bias, Wg, Wu, Wd, Sg, Su, Sd):
        import jax, jax.numpy as jnp
        import numpy as np
        H = 512
        I = 256
        E = 16
        TOPK = 4
        SI = 256
        orig_shape = hidden_states.shape
        x = hidden_states.reshape(-1, orig_shape[-1])
        scores = jax.nn.sigmoid(x @ gate_w.T) + bias
        topk_w, topk_idx = jax.lax.top_k(scores, TOPK)
        topk_w = topk_w / (jnp.sum(topk_w, axis=-1, keepdims=True) + 1e-20)
        cw = jnp.sum(jax.nn.one_hot(topk_idx, E, dtype=x.dtype) * topk_w[..., None], axis=1)
        g = jnp.einsum('th,eih->eti', x, Wg)
        u = jnp.einsum('th,eih->eti', x, Wu)
        z = jax.nn.silu(g) * u
        zw = z * cw.T[:, :, None]
        out = jnp.einsum('eti,ehi->th', zw, Wd)
        out = out + jax.nn.silu(x @ Sg.T) * (x @ Su.T) @ Sd.T
        return out.reshape(orig_shape)
    x = x + _L0_xattn_ref(_layernorm(x, axis=-1), ctx_4096, L0_xattn_Wq_d, L0_xattn_W_qk, L0_xattn_Wkv_d, L0_xattn_Wv_u)
    x = x + _L0_ffn_ref(_layernorm(x, axis=-1), L0_ffn_gate_w, L0_ffn_base_w, L0_ffn_base_b, L0_ffn_lora_A, L0_ffn_lora_B)
    x = x + _L1_xattn_ref(_layernorm(x, axis=-1), ctx_4096, mask_1x1xSxS2_ff0, L1_xattn_Wq, L1_xattn_Wk, L1_xattn_Wv, L1_xattn_Wo, L1_xattn_q_norm_w, L1_xattn_k_norm_w)
    x = x + _L1_ffn_ref(_layernorm(x, axis=-1), L1_ffn_gate_w, L1_ffn_bias, L1_ffn_Wg, L1_ffn_Wu, L1_ffn_Wd, L1_ffn_Sg, L1_ffn_Su, L1_ffn_Sd)
    return x

_drawn_inputs = setup_inputs


def setup_inputs(seed=0):
    import zlib

    import numpy as np

    out = dict(_drawn_inputs(seed))
    spreads = {'L1_xattn_q_norm_w': (1.0, 0.6),
     'L1_xattn_k_norm_w': (1.0, 0.6),
     'L1_ffn_bias': (0.0, 0.782)}
    factors = {'L0_ffn_base_b': 3.824,
     'L1_ffn_gate_w': 5.285,
     'L1_ffn_Wg': 4.224,
     'L1_ffn_Wu': 4.147,
     'L1_ffn_Wd': 4.138,
     'L1_ffn_Sg': 3.107,
     'L1_ffn_Su': 2.831,
     'L1_ffn_Sd': 2.818}
    for name, (base, spread) in spreads.items():
        noise = np.random.default_rng([zlib.crc32(name.encode()), seed]).standard_normal(out[name].shape)
        drawn = base * np.exp(spread * noise) if base else spread * noise
        out[name] = jnp.asarray(drawn.astype(out[name].dtype))
    for name, factor in factors.items():
        out[name] = (out[name] * factor).astype(out[name].dtype)
    return out
```

```python
from contextlib import ExitStack

import concourse.bass as bass
from concourse import mybir

F32 = mybir.dt.float32
F32R = mybir.dt.float32r
ALU = mybir.AluOpType
ACT = mybir.ActivationFunctionType
AX_X = mybir.AxisListType.X

P = 128
B, S, D = 4, 256, 512
NK = 1601
NKP = NK + 1
KT = D // P
QT = S // P
TT = -(-NK // P)
LAST = NK - (TT - 1) * P
STEPS = -(-TT // 2)
H0, LQ, LKV = 16, 64, 32
E0, R0 = 8, 16
KVH, GRP, HD = 8, 4, 128
E1, INNER, TOPK = 16, 256, 4
TOK = B * S // P
BLK0 = H0 // GRP
BLKS = BLK0 + KVH
UNITS = BLKS * GRP
EPS = 1e-5
NEG = -3.0e38
CHUNKS = [(0, 512), (512, 288), (800, 512), (1312, 290)]
HALVES = [(0, 800), (800, 801)]
AG = E0 * R0 + E0


def keys_in(t):
    return P if t < TT - 1 else LAST


def xattn_ffn_kernel(nc, x, ctx_t, mask, wqd, wqk, wdkv, wvu, ag_t, base_t, base_b, lora_b, wk, wv, wq, wo,
                     norms, gate_t, gate_bias, wg, wu, wd, out, x_mid):
    with ExitStack() as ctx:
        def sem(name):
            return ctx.enter_context(nc.semaphore(name))

        R_COLS, F_COLS = 35732, 17470
        arena_r = ctx.enter_context(nc.sbuf_tensor("arena_r", [P, R_COLS], F32R))
        arena_f = ctx.enter_context(nc.sbuf_tensor("arena_f", [P, F_COLS], F32))
        ps = ctx.enter_context(nc.psum_tensor("ps", [P, 8, 512], F32))
        top = {"r": 0, "f": 0}

        def take(which, *dims, at=None):
            n = 1
            for d in dims:
                n *= d
            arena = arena_r if which == "r" else arena_f
            if at is None:
                at = top[which]
                top[which] += n
            assert at + n <= (R_COLS if which == "r" else F_COLS), (which, at + n)
            v = arena[:, at:at + n]
            if len(dims) == 2:
                v = v.rearrange("p (a b) -> p a b", b=dims[1])
            if len(dims) == 3:
                v = v.rearrange("p (a b c) -> p a b c", b=dims[1], c=dims[2])
            return v

        def raw(v):
            return v.bitcast(F32)

        ctx_hl = [take("r", KT, NKP) for _ in range(2)]
        wkv_hl = [take("r", 2, KT, HD) for _ in range(2)]
        wq_hl = [take("r", 2, KT, 2 * HD) for _ in range(2)]
        wo_hl = [take("r", 2, D) for _ in range(2)]
        kT_hl = [take("r", NKP) for _ in range(2)]
        v_hl = [take("r", TT, P) for _ in range(2)]
        xnT_hl = [take("r", KT, S) for _ in range(2)]
        qT_hl = [take("r", GRP, S) for _ in range(2)]
        pT_hl = [take("r", 2, 512) for _ in range(2)]
        uT_hl = [take("r", 2, S) for _ in range(2)]
        wdkv_hl = [take("r", KT, P) for _ in range(2)]
        k0 = kT_hl[0]
        v0 = v_hl[0]
        q0 = qT_hl[0]

        p_at = top["f"]
        probs = take("f", 2, QT, NKP)
        ctx_raw = [take("f", NK, at=p_at + i * NKP) for i in range(KT)]
        base_sb = take("f", KT, D, at=p_at)
        ag_sb = take("f", KT, AG, at=p_at + 2048)
        lorab_sb = take("f", D, at=p_at + 2592)
        baseb_sb = take("f", D, at=p_at + 3104)
        lw = take("f", QT, P, at=p_at + 3616)
        lwT = take("f", QT, P, at=p_at + 3872)
        xnT_f = take("f", KT, S, at=p_at + 4 * NKP - KT * S)
        mask_sb = take("f", QT, NK)
        xb = take("f", QT, D)
        nat = take("f", QT, D)
        raw_w = take("f", 2, 1024)
        knat = take("f", 4, P)
        u0 = take("f", 2, S, at=top["f"] - 512)
        cqT = take("f", S)
        wqk_sb = take("f", GRP, P)
        wvu_sb = take("f", D)
        wqd_sb = take("f", KT, LQ)
        const_at = top["f"]
        ident = take("f", P)
        ones = take("f", P)
        junk = take("f", 2, P)
        norm_w = take("f", 2)
        half_exp = take("f", 16)
        zero = take("f", 1)
        tri = take("f", E1, E1)
        cmp0 = [take("f", QT * E0 * E0) for _ in range(2)]
        ssq = take("f", TT)
        mid = take("f", 16)
        rk = take("f", TT)
        qss = take("f", QT * GRP)
        rq = take("f", QT * GRP)
        mx = take("f", 2, QT)
        mx_a = take("f", 2, QT)
        negmax = take("f", 2, QT)
        rowsum = take("f", 2, QT)
        rinv = take("f", 2, QT)
        stats = take("f", TOK, 6)
        mv = take("f", TOK, 2)
        rstd = take("f", TOK)
        gate = take("f", QT, E0)
        g_e = take("f", QT, E0)
        g_rank = take("f", QT, E0)
        g_a = take("f", QT, E0)
        g_m = take("f", QT)
        g_sum = take("f", QT)

        def s_half(h, n):
            return ps[:, 2 * h:2 * h + 2, :].rearrange("p a b -> p (a b)")[:, 0:n]

        def strided(view, off, *dims):
            a = view[:, off:off + 1]
            return bass.AP(tensor=a.tensor, offset=a.offset, ap=[list(a.ap[0])] + [list(d) for d in dims])

        def step_cols(k):
            return (P, slice(0, 512)) if k < STEPS - 1 else (LAST, slice(0, S))

        LOW, RES, TRN = (0, 1), (2, 3), (6, 7)
        SCORE_STEPS = {0: (0, 0), 1: (0, 1), 3: (1, 0), 4: (1, 1)}
        EXP_STEPS = {2: 0, 5: 1}
        OUT_STEPS = {2: 0, 5: 1}
        Q_AT, K_LAG = 2, 4

        T, Y, U = (4, 5), 6, 7

        dma_const = sem("dma_const")
        dma_ctx = [sem(f"dma_ctx{i}") for i in range(KT)]
        dma_x = sem("dma_x")
        dma_x_out = sem("dma_x_out")
        dma_wqk = sem("dma_wqk")
        dma_ffn = sem("dma_ffn")
        dma_raw = [sem(f"dma_raw{i}") for i in range(2)]
        dma_out = sem("dma_out")
        pool_const = sem("pool_const")
        pool_split = sem("pool_split")
        pool_tmp = sem("pool_tmp")
        pool_rstd = sem("pool_rstd")
        pool_rq = sem("pool_rq")
        pool_rk = sem("pool_rk")
        act_ctx = sem("act_ctx")
        dve_ctx = sem("dve_ctx")
        dve_stat = sem("dve_stat")
        dve_var = sem("dve_var")
        dve_xn = sem("dve_xn")
        pe_xn = sem("pe_xn")
        act_xnT = sem("act_xnT")
        dve_xnT = sem("dve_xnT")
        pe_cq = sem("pe_cq")
        dve_cq = sem("dve_cq")
        pe_k0 = sem("pe_k0")
        act_k0 = sem("act_k0")
        dve_k0 = sem("dve_k0")
        pe_v0 = sem("pe_v0")
        act_v0 = sem("act_v0")
        pe_q0 = sem("pe_q0")
        act_q0 = sem("act_q0")
        dve_q0 = sem("dve_q0")
        pe_q = sem("pe_q")
        act_qss = sem("act_qss")
        dve_qn = sem("dve_qn")
        pe_qT = sem("pe_qT")
        act_qT = sem("act_qT")
        dve_qT = sem("dve_qT")
        pe_kv = sem("pe_kv")
        act_kss = sem("act_kss")
        act_v = sem("act_v")
        dve_v = sem("dve_v")
        dve_kn = sem("dve_kn")
        pe_kT = sem("pe_kT")
        pe_knat = sem("pe_knat")
        act_kT = sem("act_kT")
        dve_kT = sem("dve_kT")
        pe_s = sem("pe_s")
        dve_s = sem("dve_s")
        dve_max = sem("dve_max")
        act_p = sem("act_p")
        pe_pT = sem("pe_pT")
        act_pT = sem("act_pT")
        dve_pT = sem("dve_pT")
        pe_av = sem("pe_av")
        act_u = sem("act_u")
        dve_u = sem("dve_u")
        dve_rinv = sem("dve_rinv")
        pe_y = sem("pe_y")
        dve_y = sem("dve_y")
        pe_low = sem("pe_low")
        pe_res = sem("pe_res")
        act_ge = sem("act_ge")
        dve_gate = sem("dve_gate")
        dve_lw = sem("dve_lw")
        pe_lw = sem("pe_lw")
        act_lw = sem("act_lw")
        dve_ffn = sem("dve_ffn")
        dve_link = sem("dve_link")
        dve_cmp = sem("dve_cmp")
        dve_w = sem("dve_w")
        pool_wo = sem("pool_wo")
        alone = {e.engine: sem(f"alone_{n}") for n, e in (("pe", nc.tensor), ("dve", nc.vector),
                                                          ("pool", nc.gpsimd))}
        dma_xall = sem("dma_xall")
        dma_gate = sem("dma_gate")
        dve_xnat = sem("dve_xnat")
        pe_mx = sem("pe_mx")
        act_xhi = sem("act_xhi")
        act_xg = sem("act_xg")
        dve_xlo = sem("dve_xlo")
        pe_lg = sem("pe_lg")
        act_lg = sem("act_lg")
        dve_cw = sem("dve_cw")
        pe_gu = sem("pe_gu")
        act_sil = sem("act_sil")
        dve_z = sem("dve_z")
        act_z = sem("act_z")
        dve_zl = sem("dve_zl")
        pe_dn = sem("pe_dn")
        dve_dn = sem("dve_dn")

        S0, PT0, PP0, AV0, U0_, Z0, DN0, Y0, Q0, X0 = 2, 2, STEPS + 1, 2, 2, 2, 4, 1, 1, 16
        LN_PER_B = 3
        SPLIT0, SPLITB = 5, 6

        xnT_all = [take("r", KT, TOK * P, at=i * KT * TOK * P) for i in range(2)]
        er_at = 2 * KT * TOK * P
        E_R = 2 * KT * INNER + 2 * D
        ew = [[take("r", E_R, at=er_at + (2 * b + i) * E_R) for i in range(2)] for b in range(2)]
        z_hl = [take("r", 2, TOK * P, at=er_at + 4 * E_R + i * 2 * TOK * P) for i in range(2)]

        def gu_w(buf, part, which):
            return ew[buf][part][:, which * KT * INNER:(which + 1) * KT * INNER].rearrange(
                "p (k i) -> p k i", i=INNER)

        def dn_w(buf, part):
            return ew[buf][part][:, 2 * KT * INNER:].rearrange("p (k n) -> p k n", n=D)

        f_at = 0
        x_all = take("f", TOK, D, at=0)
        raw_e = [take("f", E_R, at=TOK * D + i * E_R) for i in range(2)]
        m_at = TOK * D + 2 * E_R
        sil = take("f", 2, 512, at=m_at)
        zf = take("f", 2, 512, at=m_at + 1024)
        xnat = [take("f", D, at=m_at + i * D) for i in range(2)]
        xnT_g = [take("f", KT, P, at=m_at + 1024 + i * 512) for i in range(2)]
        gate_sb = take("f", KT, E1, at=m_at + 2048)
        bias_sb = take("f", E1, at=m_at + 2112)
        sc = take("f", TOK, E1, at=m_at + 2128)
        cw = take("f", TOK, E1 + 1, at=m_at + 2256)
        rank = take("f", TOK, E1, at=m_at + 2400)
        wsum = take("f", TOK, at=m_at + 2528)
        cmp1 = [take("f", TOK * E1 * E1, at=m_at), take("f", TOK * E1 * E1, at=m_at + 2540)]
        assert m_at + 2540 + TOK * E1 * E1 <= const_at

        CONSTS = 11

        def wait_alone(eng, *waits):
            for s_, value in waits:
                eng.wait_ge(s_, value)
            eng.sem_inc(alone[eng.engine], 1)

        block = ctx.enter_context(nc.Block())

        @block.sync
        def _(sp):
            sp.sem_inc(dma_x_out, X0)
            for dst, src in ((mask_sb, mask.rearrange("t p k -> p t k")), (wqd_sb, wqd), (wvu_sb, wvu),
                             (norm_w, norms)):
                sp.dma_start(dst, src).then_inc(dma_const, 16)

            def load(n, slot, dst, src):
                sp.wait_ge(pool_split, n - 1)
                sp.dma_start(dst, src).then_inc(dma_raw[slot], 16)

            def kv_part(slot):
                return raw_w[:, slot, 0:KT * HD].rearrange("p (k d) -> p k d", d=HD)

            sp.dma_start(kv_part(0), wdkv).then_inc(dma_raw[0], 16)
            sp.dma_start(kv_part(1), wk[0]).then_inc(dma_raw[1], 16)
            load(2, 0, kv_part(0), wv[0])
            load(3, 1, raw_w[:, 1, :], wq[0, 0])
            load(4, 0, raw_w[:, 0, :], wq[0, 1])
            with sp.Fori(0, B) as b:
                sp.wait_ge(pe_pT, b * (UNITS * STEPS) + PP0)
                for k in range(KT):
                    sp.dma_start(ctx_raw[k], ctx_t[b, k]).then_inc(dma_ctx[k], 16)
                sp.wait_ge(dma_x_out, b * 16 + X0)
                sp.dma_start(xb, x[b].rearrange("t p d -> p t d")).then_inc(dma_x, 16)
                with sp.Fori(0, BLK0) as k:
                    sp.wait_ge(pe_q0, b * BLK0 + k + Q0)
                    sp.dma_start(wqk_sb[0:LQ], wqk[k]).then_inc(dma_wqk, 16)
                sp.wait_ge(pe_pT, b * (UNITS * STEPS) + H0 * STEPS + PP0)
                for dst, src in ((base_sb, base_t), (ag_sb, ag_t), (lorab_sb, lora_b),
                                 (baseb_sb[0:1], base_b)):
                    sp.dma_start(dst, src).then_inc(dma_ffn, 16)
                with sp.Fori(0, KVH) as g:
                    n = b * (KVH * SPLITB) + g * SPLITB + SPLIT0
                    load(n, 1, raw_w[:, 1, :], wo[g, 0])
                    load(n + 1, 0, kv_part(0), wk[g + 1])
                    load(n + 2, 1, kv_part(1), wv[g + 1])
                    load(n + 3, 0, raw_w[:, 0, :], wo[g, 1])
                    load(n + 4, 1, raw_w[:, 1, :], wq[g + 1, 0])
                    load(n + 5, 0, raw_w[:, 0, :], wq[g + 1, 1])
                sp.wait_ge(dve_y, (b + 1) * (UNITS * QT) + Y0)
                sp.dma_start(x_mid[b].rearrange("t p d -> p t d"), xb).then_inc(dma_x_out, 16)
            sp.wait_ge(dma_x_out, B * 16 + X0)
            sp.wait_ge(pe_y, B * UNITS * QT)
            sp.dma_start(x_all.rearrange("p (b t) d -> p b t d", t=QT),
                         x_mid.rearrange("b t p d -> p b t d")).then_inc(dma_xall, 16)
            sp.wait_ge(pool_split, B * KVH * SPLITB + SPLIT0)
            sp.dma_start(gate_sb, gate_t).then_inc(dma_gate, 16)
            sp.dma_start(bias_sb, gate_bias).then_inc(dma_gate, 16)
            base = B * KVH * SPLITB + SPLIT0

            def load_expert(e, slot):
                n = KT * INNER
                sp.dma_start(raw_e[slot][:, 0:n], wg[e]).then_inc(dma_raw[slot], 16)
                sp.dma_start(raw_e[slot][:, n:2 * n], wu[e]).then_inc(dma_raw[slot], 16)
                sp.dma_start(raw_e[slot][:, 2 * n:], wd[e]).then_inc(dma_raw[slot], 16)

            load_expert(0, 0)
            load_expert(1, 1)
            with sp.Fori(0, E1 // 2 - 1) as i:
                for j in range(2):
                    sp.wait_ge(pool_split, i * 2 + (base + 1 + j))
                    load_expert(i * 2 + (2 + j), j)
            sp.wait_ge(pool_split, base + E1 - 1)
            load_expert(E1, 0)
            sp.wait_ge(dve_dn, (E1 + 1) * TOK + DN0)
            sp.dma_start(out.rearrange("b t p d -> p b t d"),
                         x_all.rearrange("p (b t) d -> p b t d", t=QT)).then_inc(dma_out, 16)
            sp.wait_ge(dma_out, 16)

        @block.gpsimd
        def _(pool):
            def step(ins):
                ins.then_inc(pool_const, 1)

            step(pool.memset(ident, 0.0))
            step(pool.memset(ones, 1.0))
            step(pool.memset(half_exp, -0.5))
            step(pool.memset(tri, 1.0))
            step(pool.memset(zero, 0.0))
            step(pool.memset(raw(ctx_hl[0][:, :, NK:NKP]), 0.0))
            step(pool.memset(raw(ctx_hl[1][:, :, NK:NKP]), 0.0))
            step(pool.memset(raw(kT_hl[0][:, NK:NKP]), 0.0))
            step(pool.memset(raw(kT_hl[1][:, NK:NKP]), 0.0))
            pool.wait_ge(pool_const, CONSTS - 2)
            step(pool.affine_select(out=ident, in_=ident, compare_op=ALU.not_equal, fill=1.0, base=0,
                                    pattern=[[-1, P]], channel_multiplier=1))
            step(pool.affine_select(out=tri, in_=tri, compare_op=ALU.is_gt, fill=0.0, base=0,
                                    pattern=[[1, E1], [-1, E1]], channel_multiplier=0))

            pool.wait_ge(pool_const, CONSTS)

            def kv_raw(slot):
                return raw_w[:, slot, 0:KT * HD].rearrange("p (k d) -> p k d", d=HD)

            def q_raw(slot):
                return raw_w[:, slot, :].rearrange("p (k d) -> p k d", d=2 * HD)

            def split_chunk(slot, loads, dsts, src, hi_n):
                pool.wait_ge(dma_raw[slot], loads)
                wait_alone(pool)
                pool.tensor_copy(dsts[0], src).then_inc(pool_tmp, 1)
                pool.wait_ge(pool_tmp, hi_n)
                return pool.tensor_tensor(dsts[1], src, raw(dsts[0]), ALU.subtract)

            def pick(hl, *idx):
                return [hl[0][idx], hl[1][idx]]

            every = slice(None)
            split_chunk(0, 16, wdkv_hl, kv_raw(0), 1).then_inc(pool_split, 1)
            split_chunk(1, 16, pick(wkv_hl, every, 0), kv_raw(1), 2).then_inc(pool_split, 1)
            split_chunk(0, 32, pick(wkv_hl, every, 1), kv_raw(0), 3).then_inc(pool_split, 1)
            split_chunk(1, 32, pick(wq_hl, every, 0), q_raw(1), 4).then_inc(pool_split, 1)
            split_chunk(0, 48, pick(wq_hl, every, 1), q_raw(0), 5).then_inc(pool_split, 1)

            TMP_BLK = 1 + TT + SPLITB + 2
            TMP_B = LN_PER_B + KVH * TMP_BLK

            def inverse_root(dst, src, mul, add, tmp_n):
                wait_alone(pool)
                n = dst.shape[-1]
                pool.tensor_scalar(mid[:, 0:n], src, mul, add, ALU.mult, ALU.add).then_inc(pool_tmp, 1)
                pool.wait_ge(pool_tmp, tmp_n)
                return pool.tensor_tensor(dst, mid[:, 0:n], half_exp[:, 0:n], ALU.pow)

            with pool.Fori(0, B) as b:
                for ln in range(LN_PER_B):
                    tmp_n = b * TMP_B + (5 + ln + 1)
                    pool.wait_ge(dve_var, b * (LN_PER_B * QT) + (ln + 1) * QT)
                    inverse_root(rstd[:, 0:QT], mv[:, 0:QT, 1], 1.0, EPS, tmp_n).then_inc(pool_rstd, 1)
                    pool.wait_ge(pool_rstd, b * LN_PER_B + (ln + 1))
                wait_alone(pool)
                with pool.Fori(0, KVH) as g:
                    blk = b * KVH + g
                    t0 = b * TMP_B + g * TMP_BLK + (5 + LN_PER_B)
                    pool.wait_ge(act_qss, blk * (QT * GRP) + QT * GRP)
                    inverse_root(rq, qss, 1.0, HD * EPS, t0 + 1).then_inc(pool_rq, 1)
                    pool.wait_ge(pool_rq, blk + 1)
                    for t in range(TT):
                        n = keys_in(t)
                        wait_alone(pool, (act_kss, blk * TT + (t + 1)))
                        pool.tensor_scalar(mid[0:n, 0:1], ssq[0:n, t:t + 1], 1.0 / HD, EPS, ALU.mult,
                                           ALU.add).then_inc(pool_tmp, 1)
                        pool.wait_ge(pool_tmp, t0 + (t + 2))
                        pool.tensor_tensor(rk[0:n, t:t + 1], mid[0:n, 0:1], half_exp[0:n, 0:1],
                                           ALU.pow).then_inc(pool_rk, 1)
                        pool.wait_ge(pool_rk, blk * TT + (t + 1))
                    ld = blk * (3 * 16)
                    m = t0 + (1 + TT)

                    def split_o(pair, slot, loads, m):
                        for i in range(2):
                            j = 2 * pair + i
                            head = b * UNITS + g * GRP + (H0 + j)
                            pool.wait_ge(pe_y, head * QT - QT)
                            ins = split_chunk(slot, loads, pick(wo_hl, every, i),
                                              raw_w[:, slot, i * D:(i + 1) * D], m + (i + 1))
                            ins.then_inc(pool_wo, 1)
                        return ins

                    split_o(0, 1, ld + 48, m)
                    pool.wait_ge(pool_wo, blk * GRP + 2)
                    pool.sem_inc(pool_split, 1)
                    pool.wait_ge(pe_kv, blk * TT + TT)
                    split_chunk(0, ld + 64, pick(wkv_hl, every, 0), kv_raw(0), m + 3).then_inc(pool_split, 1)
                    split_chunk(1, ld + 64, pick(wkv_hl, every, 1), kv_raw(1), m + 4).then_inc(pool_split, 1)
                    split_o(1, 0, ld + 80, m + 4)
                    pool.wait_ge(pool_wo, blk * GRP + 4)
                    pool.sem_inc(pool_split, 1)
                    split_chunk(1, ld + 80, pick(wq_hl, every, 0), q_raw(1), m + 7).then_inc(pool_split, 1)
                    split_chunk(0, ld + 96, pick(wq_hl, every, 1), q_raw(0), m + 8).then_inc(pool_split, 1)

            t1 = 5 + B * TMP_B
            pool.wait_ge(dve_var, B * LN_PER_B * QT + TOK)
            inverse_root(rstd, mv[:, :, 1], 1.0, EPS, t1 + 1).then_inc(pool_rstd, 1)
            pool.wait_ge(pe_y, B * UNITS * QT)

            def split_expert(e, slot, loads, tmp_n):
                pool.wait_ge(dma_raw[slot], loads)
                wait_alone(pool)
                pool.tensor_copy(ew[slot][0], raw_e[slot]).then_inc(pool_tmp, 1)
                pool.wait_ge(pool_tmp, tmp_n)
                pool.tensor_tensor(ew[slot][1], raw_e[slot], raw(ew[slot][0]),
                                   ALU.subtract).then_inc(pool_split, 1)

            had = [16 * (3 + 3 * B * KVH), 16 * (2 + 3 * B * KVH)]
            for e in range(2):
                split_expert(e, e, had[e] + 48, t1 + 2 + e)
            with pool.Fori(0, E1 // 2 - 1) as i:
                for j in range(2):
                    pool.wait_ge(pe_dn, i * (2 * TOK) + (j + 1) * TOK)
                    split_expert(None, j, i * 48 + (had[j] + 96), i * 2 + (t1 + 4 + j))
            pool.wait_ge(pe_dn, (E1 - 1) * TOK)
            split_expert(None, 0, had[0] + 48 * 9, t1 + 2 + E1)

        def unit_mm(pe, dst, left, right, parts, start, stop):
            for n, (a, c) in enumerate(parts):
                ins = pe.matmul(dst, left[a], right[c], start=start and n == 0,
                                stop=stop and n == len(parts) - 1)
            return ins

        THREE = ((0, 0), (0, 1), (1, 0))

        @block.tensor
        def _(pe):
            pe.sem_inc(pe_pT, PP0)
            pe.sem_inc(pe_av, AV0)
            pe.sem_inc(pe_q0, Q0)
            pe.wait_ge(pool_const, CONSTS)
            pe.wait_ge(dma_const, 64)

            def transpose_x(ln):
                pe.wait_ge(dve_xn, ln * QT + QT)
                for k in range(KT):
                    for q in range(QT):
                        c = (k % 2) * S + q * P
                        ins = pe.transpose(ps[:, T[k // 2], c:c + P], nat[:, q, k * P:(k + 1) * P], ident)
                    if k % 2:
                        ins.then_inc(pe_xn, 1)

            def units(u0_, layer, b, blk_in_b):
                def scores(j, q, h):
                    u = u0_ + j
                    pe.wait_ge(dve_s, u * 4 + (2 * q + h + 1 - 2 + S0))
                    for i in range(2):
                        c0, n = CHUNKS[2 * h + i]
                        dst = ps[:, 2 * h + i, 0:n]
                        qs = slice(q * P, (q + 1) * P)
                        if layer == 0:
                            ins = pe.matmul(dst, q0[:, j, qs], k0[:, c0:c0 + n], start=True, stop=True)
                        else:
                            ins = unit_mm(pe, dst, [v[:, j, qs] for v in qT_hl],
                                          [v[:, c0:c0 + n] for v in kT_hl], THREE, True, True)
                    ins.then_inc(pe_s, 1)

                def transposes(j, k):
                    u = u0_ + j
                    if k == 0:
                        pe.wait_ge(act_p, u * QT + QT)
                    pe.wait_ge(dve_pT, u * STEPS + (k + 1 - 2 + PT0))
                    for i in range(min(2, TT - 2 * k)):
                        t = 2 * k + i
                        n = keys_in(t)
                        for q in range(QT):
                            c = i * S + q * P
                            ins = pe.transpose(ps[0:n, T[(j + k) % 2], c:c + P],
                                               probs[:, j % 2, q, t * P:t * P + n], ident)
                    ins.then_inc(pe_pT, 1)

                def values(j, k):
                    u = u0_ + j
                    pe.wait_ge(dve_pT, u * STEPS + (k + 1 + PT0))
                    if k == 0:
                        pe.wait_ge(dve_u, u + (1 - 2 + U0_))
                    dst = ps[:, U, (j % 2) * S:(j % 2 + 1) * S]
                    for i in range(min(2, TT - 2 * k)):
                        t = 2 * k + i
                        n = keys_in(t)
                        right = [v[0:n, (j + k) % 2, i * S:(i + 1) * S] for v in pT_hl]
                        first, last = t == 0, t == TT - 1
                        if layer == 0:
                            ins = unit_mm(pe, dst, [v0[0:n, t, :]] * 1, right, ((0, 0), (0, 1)), first, last)
                        else:
                            ins = unit_mm(pe, dst, [v[0:n, t, :] for v in v_hl], right, THREE, first, last)
                    ins.then_inc(pe_av, 1)

                def outputs(j, q):
                    u = u0_ + j
                    if q == 0:
                        pe.wait_ge(dve_u, u + (1 + U0_))
                        if layer == 1:
                            pe.wait_ge(pool_wo, (b * KVH + blk_in_b) * GRP + (j + 1))
                    pe.wait_ge(dve_y, u * QT + (q + Y0))
                    qs = slice(q * P, (q + 1) * P)
                    if layer == 0:
                        ins = pe.matmul(ps[:, Y, 0:LKV], u0[:, j % 2, qs],
                                        wvu_sb[:, bass.ds(blk_in_b * (GRP * LKV) + j * LKV, LKV)], start=True, stop=True)
                    else:
                        ins = unit_mm(pe, ps[:, Y, :], [v[:, j % 2, qs] for v in uT_hl],
                                      [v[:, j % 2, :] for v in wo_hl], THREE, True, True)
                    ins.then_inc(pe_y, 1)

                for q in range(QT):
                    for h in range(2):
                        scores(0, q, h)
                for j in range(GRP):
                    transposes(j, 0)
                    for k in range(STEPS):
                        if k + 1 < STEPS:
                            transposes(j, k + 1)
                        if j + 1 < GRP and k in SCORE_STEPS:
                            scores(j + 1, *SCORE_STEPS[k])
                        if j and k in OUT_STEPS:
                            outputs(j - 1, OUT_STEPS[k])
                        values(j, k)
                for q in range(QT):
                    outputs(GRP - 1, q)

            with pe.Fori(0, B) as b:
                transpose_x(b * LN_PER_B)
                pe.wait_ge(act_xnT, b * LN_PER_B * 2 + 2)
                for k in range(KT):
                    ins = pe.matmul(ps[0:LQ, Y, 0:S], wqd_sb[:, k, :], xnT_f[:, k, :], start=(k == 0),
                                    stop=(k == KT - 1))
                ins.then_inc(pe_cq, 1)
                pe.wait_ge(pool_split, 1)
                pe.wait_ge(dve_ctx, b * KT + KT)
                for c, (c0, n) in enumerate(CHUNKS):
                    for k in range(KT):
                        ins = unit_mm(pe, ps[:, c, 0:n], [v[:, k, :] for v in wdkv_hl],
                                      [v[:, k, c0:c0 + n] for v in ctx_hl], THREE, k == 0, k == KT - 1)
                    ins.then_inc(pe_k0, 1)
                for t in range(TT):
                    if t == 0:
                        pe.wait_ge(dve_k0, b * 4 + 4)
                    if t % 4 == 0 and t >= 8:
                        pe.wait_ge(act_v0, b * 4 + (t // 4 - 1))
                    n = keys_in(t)
                    ins = pe.transpose(ps[0:n, T[t // 4 % 2], (t % 4) * P:(t % 4 + 1) * P],
                                       raw(k0[:, t * P:t * P + n]), ident)
                    if t % 4 == 3 or t == TT - 1:
                        ins.then_inc(pe_v0, 1)
                pe.wait_ge(act_v0, b * 4 + 4)
                wait_alone(pe, (dve_cq, b + 1))
                with pe.Fori(0, BLK0) as k:
                    blk = b * BLK0 + k
                    u0_ = b * UNITS + k * GRP
                    pe.wait_ge(dma_wqk, blk * 16 + 16)
                    pe.wait_ge(dve_pT, u0_ * STEPS + PT0)
                    for j in range(GRP):
                        ins = pe.matmul(ps[:, T[j // 2], (j % 2) * S:(j % 2 + 1) * S], wqk_sb[0:LQ, j, :],
                                        cqT[0:LQ, :], start=True, stop=True)
                    ins.then_inc(pe_q0, 1)
                    pe.wait_ge(dve_q0, blk * 4 + 4)
                    units(u0_, 0, b, k)

                transpose_x(b * LN_PER_B + 1)
                pe.wait_ge(act_xnT, b * LN_PER_B * 2 + 4)
                pe.wait_ge(dma_ffn, b * 64 + 64)
                for q in range(QT):
                    qs = slice(q * P, (q + 1) * P)
                    for k in range(KT):
                        ins = pe.matmul(ps[:, LOW[q], 0:AG], xnT_f[:, k, qs], ag_sb[:, k, :],
                                        start=(k == 0), stop=(k == KT - 1))
                    ins.then_inc(pe_low, 1)
                for q in range(QT):
                    qs = slice(q * P, (q + 1) * P)
                    for k in range(KT):
                        pe.matmul(ps[:, RES[q], :], xnT_f[:, k, qs], base_sb[:, k, :], start=(k == 0),
                                  stop=False)
                    pe.matmul(ps[:, RES[q], :], ones[0:1, :], baseb_sb[0:1, :], start=False, stop=False)
                for q in range(QT):
                    pe.wait_ge(dve_lw, b * QT + (q + 1))
                    pe.transpose(ps[:, TRN[q], 0:P], lw[:, q, :], ident).then_inc(pe_lw, 1)
                for q in range(QT):
                    pe.wait_ge(act_lw, b * QT + (q + 1))
                    pe.matmul(ps[:, RES[q], :], lwT[:, q, :], lorab_sb, start=False,
                              stop=True).then_inc(pe_res, 1)

                transpose_x(b * LN_PER_B + 2)
                wait_alone(pe, (dve_xnT, b * 2 + 2))
                with pe.Fori(0, KVH) as g:
                    blk = b * KVH + g
                    u0_ = b * UNITS + g * GRP + H0
                    pe.wait_ge(pool_split, blk * SPLITB + SPLIT0)
                    pe.wait_ge(dve_y, u0_ * QT + Y0)
                    for q in range(QT):
                        for pair in range(2):
                            for k in range(KT):
                                ins = unit_mm(pe, ps[:, (Y, U)[q], pair * S:(pair + 1) * S],
                                              [v[:, k, q * P:(q + 1) * P] for v in xnT_hl],
                                              [v[:, pair, k, :] for v in wq_hl], THREE, k == 0,
                                              k == KT - 1)
                        ins.then_inc(pe_q, 1)

                    def kv_tile(t):
                        if t >= 4:
                            pe.wait_ge(dve_kn, blk * TT + (t - 3))
                            pe.wait_ge(dve_v, blk * TT + (t - 3))
                        n = keys_in(t)
                        dst = ps[0:n, t % 4, 0:2 * HD].rearrange("p (w d) -> p w d", d=HD)
                        for k in range(KT):
                            ins = unit_mm(pe, dst, [v[:, k, t * P:t * P + n] for v in ctx_hl],
                                          [v[:, :, k, :] for v in wkv_hl], THREE, k == 0, k == KT - 1)
                        ins.then_inc(pe_kv, 1)

                    def k_transpose(t):
                        pe.wait_ge(dve_kn, blk * TT + (t + 1))
                        c = t // 4
                        if t % 4 == 0:
                            if c < 2:
                                pe.wait_ge(dve_qT, blk * 2 + 2)
                            else:
                                pe.wait_ge(dve_kT, blk * 4 + (c - 1))
                        n = keys_in(t)
                        ins = pe.transpose(ps[:, T[c % 2], (t % 4) * P:(t % 4) * P + n],
                                           knat[0:n, t % 4, :], ident[0:n, 0:n])
                        ins.then_inc(pe_knat, 1)

                    for t in range(TT):
                        kv_tile(t)
                        if t == Q_AT:
                            pe.wait_ge(dve_qn, blk * QT + QT)
                            pe.wait_ge(dve_pT, u0_ * STEPS + PT0)
                            for j in range(GRP):
                                for q in range(QT):
                                    c = (j % 2) * S + q * P
                                    ins = pe.transpose(ps[:, T[j // 2], c:c + P],
                                                       nat[:, q, j * P:(j + 1) * P], ident)
                                if j % 2:
                                    ins.then_inc(pe_qT, 1)
                        if t >= K_LAG:
                            k_transpose(t - K_LAG)
                    for t in range(TT - K_LAG, TT):
                        k_transpose(t)
                    pe.wait_ge(dve_kT, blk * 4 + 4)
                    units(u0_, 1, b, g)

            for t in range(TOK):
                pe.wait_ge(dve_xnat, t + 1)
                if t >= 2:
                    pe.wait_ge(dve_xlo, t - 1)
                    pe.wait_ge(act_xg, t - 1)
                for k in range(KT):
                    ins = pe.transpose(ps[:, T[t % 2], k * P:(k + 1) * P],
                                       xnat[t % 2][:, k * P:(k + 1) * P], ident)
                ins.then_inc(pe_mx, 1)
                pe.wait_ge(act_xg, t + 1)
                if t == 0:
                    pe.wait_ge(dma_gate, 32)
                for k in range(KT):
                    ins = pe.matmul(ps[:, Y, t * E1:(t + 1) * E1], xnT_g[t % 2][:, k, :], gate_sb[:, k, :],
                                    start=(k == 0), stop=(k == KT - 1))
                ins.then_inc(pe_lg, 1)
            pe.wait_ge(dve_xlo, TOK)
            pe.wait_ge(act_lg, 1)
            pe.wait_ge(dve_cw, 1)
            base = B * KVH * SPLITB + SPLIT0

            def expert(e, buf):
                pe.wait_ge(pool_split, base + 1 + e)
                for c in range(2):
                    for it in range(2):
                        n = 2 * c + it
                        pe.wait_ge(dve_z, e * 4 + (n + 1 - 2 + Z0))
                        for which in range(2):
                            w = [gu_w(buf, part, which) for part in range(2)]
                            for k in range(KT):
                                ins = unit_mm(pe, ps[:, 2 * (n % 2) + which, :],
                                              [v[:, k, it * P:(it + 1) * P] for v in w],
                                              [v[:, k, c * 512:(c + 1) * 512] for v in xnT_all], THREE,
                                              k == 0, k == KT - 1)
                        ins.then_inc(pe_gu, 1)
                for t in range(TOK):
                    pe.wait_ge(dve_zl, e * 4 + ((2 if t < TOK // 2 else 4) + Z0))
                    pe.wait_ge(dve_dn, e * TOK + (t + 1 - 4 + DN0))
                    for it in range(2):
                        ins = unit_mm(pe, ps[:, 4 + t % 4, :], [v[:, it, t * P:(t + 1) * P] for v in z_hl],
                                      [dn_w(buf, part)[:, it, :] for part in range(2)], THREE, it == 0,
                                      it == 1)
                    ins.then_inc(pe_dn, 1)

            with pe.Fori(0, E1 // 2) as i:
                expert(i * 2, 0)
                expert(i * 2 + 1, 1)
            expert(E1, 0)

        @block.scalar
        def _(act):
            act.preload_act_table(ACT.Exp)

            def copy(dst, src, **kw):
                return act.activation(dst, src, ACT.Copy, **kw)

            def xnT_copies(ln, layer1):
                for i in range(2):
                    act.wait_ge(pe_xn, ln * 2 + (i + 1))
                    dst = (xnT_hl[0] if layer1 else xnT_f)[:, 2 * i:2 * i + 2, :]
                    copy(dst, ps[:, T[i], :].rearrange("p (k s) -> p k s", s=S)).then_inc(act_xnT, 1)

            def units(u0_, layer):
                def exps(j, q):
                    u = u0_ + j
                    act.wait_ge(dve_max, u * QT + (q + 1))
                    act.activation(probs[:, j % 2, q, 0:NK], probs[:, j % 2, q, 0:NK], ACT.Exp,
                                   bias=negmax[:, j % 2, q:q + 1],
                                   accum_out=rowsum[:, j % 2, q:q + 1]).then_inc(act_p, 1)

                def highs(j, k):
                    u = u0_ + j
                    act.wait_ge(pe_pT, u * STEPS + (k + 1 + PP0))
                    act.wait_ge(pe_av, u * STEPS + (k + 1 - 2 + AV0))
                    buf = (j + k) % 2
                    n, c = step_cols(k)
                    copy(pT_hl[0][0:n, buf, c], ps[0:n, T[buf], c]).then_inc(act_pT, 1)

                def head(j):
                    u = u0_ + j
                    act.wait_ge(pe_av, (u + 1) * STEPS + AV0)
                    src = ps[:, U, (j % 2) * S:(j % 2 + 1) * S]
                    dst = u0 if layer == 0 else uT_hl[0]
                    copy(dst[:, j % 2, :], src).then_inc(act_u, 1)

                for q in range(QT):
                    exps(0, q)
                for j in range(GRP):
                    for k in range(STEPS):
                        highs(j, k)
                        if j + 1 < GRP and k in EXP_STEPS:
                            exps(j + 1, EXP_STEPS[k])
                    head(j)

            with act.Fori(0, B) as b:
                for k in range(KT):
                    act.wait_ge(dma_ctx[k], b * 16 + 16)
                    if k == 0:
                        act.wait_ge(pe_pT, b * (UNITS * STEPS) + PP0)
                    copy(ctx_hl[0][:, k, 0:NK], ctx_raw[k]).then_inc(act_ctx, 1)
                for i in range(2):
                    act.wait_ge(pe_xn, b * (LN_PER_B * 2) + (i + 1))
                    act.wait_ge(dve_ctx, b * KT + KT)
                    copy(xnT_f[:, 2 * i:2 * i + 2, :],
                         ps[:, T[i], :].rearrange("p (k s) -> p k s", s=S)).then_inc(act_xnT, 1)
                for c, (c0, n) in enumerate(CHUNKS):
                    act.wait_ge(pe_k0, b * 4 + (c + 1))
                    n = min(n, NK - c0)
                    copy(k0[:, c0:c0 + n], ps[:, c, 0:n]).then_inc(act_k0, 1)
                for c in range(4):
                    act.wait_ge(pe_v0, b * 4 + (c + 1))
                    if c < 3:
                        copy(v0[:, 4 * c:4 * c + 4, :],
                             ps[:, T[c % 2], :].rearrange("p (t d) -> p t d", d=P)).then_inc(act_v0, 1)
                    else:
                        copy(v0[0:LAST, TT - 1, :], ps[0:LAST, T[c % 2], 0:P]).then_inc(act_v0, 1)
                with act.Fori(0, BLK0) as kk:
                    act.wait_ge(pe_q0, b * BLK0 + kk + (1 + Q0))
                    for i in range(2):
                        copy(q0[:, 2 * i:2 * i + 2, :],
                             ps[:, T[i], :].rearrange("p (k s) -> p k s", s=S),
                             scale=float(LKV) ** -0.5).then_inc(act_q0, 1)
                    units(b * UNITS + kk * GRP, 0)
                xnT_copies(b * LN_PER_B + 1, False)
                act.wait_ge(dve_gate, b + 1)
                act.activation(g_e, g_a, ACT.Exp).then_inc(act_ge, 1)
                for q in range(QT):
                    act.wait_ge(pe_lw, b * QT + (q + 1))
                    copy(lwT[:, q, :], ps[:, TRN[q], 0:P]).then_inc(act_lw, 1)
                xnT_copies(b * LN_PER_B + 2, True)
                with act.Fori(0, KVH) as g:
                    blk = b * KVH + g
                    for q in range(QT):
                        act.wait_ge(pe_q, blk * QT + (q + 1))
                        for j in range(GRP):
                            n = q * GRP + j
                            if n >= 2:
                                act.wait_ge(act_qss, blk * (QT * GRP) + (n - 1))
                            act.activation(junk[:, n % 2, :], ps[:, (Y, U)[q], j * P:(j + 1) * P],
                                           ACT.Square, accum_out=qss[:, n:n + 1]).then_inc(act_qss, 1)
                    act.wait_ge(act_qss, blk * (QT * GRP) + QT * GRP)

                    def kv(t):
                        n = keys_in(t)
                        act.wait_ge(pe_kv, blk * TT + (t + 1))
                        if t >= 2:
                            act.wait_ge(act_kss, blk * TT + (t - 1))
                        act.activation(junk[0:n, t % 2, :], ps[0:n, t % 4, 0:P], ACT.Square,
                                       accum_out=ssq[0:n, t:t + 1]).then_inc(act_kss, 1)
                        copy(v_hl[0][0:n, t, :], ps[0:n, t % 4, P:2 * P]).then_inc(act_v, 1)

                    def kT(c):
                        act.wait_ge(pe_knat, blk * TT + min(4 * c + 4, TT))
                        n = min(512, NK - 512 * c)
                        copy(kT_hl[0][:, 512 * c:512 * c + n], ps[:, T[c % 2], 0:n],
                             scale=norm_w[:, 1:2]).then_inc(act_kT, 1)

                    for t in range(TT):
                        kv(t)
                        if t == Q_AT:
                            for i in range(2):
                                act.wait_ge(pe_qT, blk * 2 + (i + 1))
                                copy(qT_hl[0][:, 2 * i:2 * i + 2, :],
                                     ps[:, T[i], :].rearrange("p (k s) -> p k s", s=S),
                                     scale=norm_w[:, 0:1]).then_inc(act_qT, 1)
                        if t >= K_LAG + 3 and (t - K_LAG - 3) % 4 == 0:
                            kT((t - K_LAG - 3) // 4)
                    for c in range(2, 4):
                        kT(c)
                    act.wait_ge(act_kss, blk * TT + TT)
                    units(b * UNITS + g * GRP + H0, 1)

            for t in range(TOK):
                act.wait_ge(pe_mx, t + 1)
                src = ps[:, T[t % 2], :].rearrange("p (k s) -> p k s", s=P)
                copy(xnT_all[0][:, :, t * P:(t + 1) * P], src).then_inc(act_xhi, 1)
                if t >= 2:
                    act.wait_ge(pe_lg, t - 1)
                copy(xnT_g[t % 2], src).then_inc(act_xg, 1)
            act.wait_ge(pe_lg, TOK)
            act.activation(sc, ps[:, Y, 0:TOK * E1].rearrange("p (t e) -> p t e", e=E1),
                           ACT.Sigmoid).then_inc(act_lg, 1)

            act.preload_act_table(ACT.Silu)

            act.sem_inc(act_z, Z0)

            def expert(e):
                def silu(n):
                    act.wait_ge(pe_gu, e * 4 + (n + 1))
                    act.wait_ge(dve_z, e * 4 + (n + 1 - 2 + Z0))
                    act.activation(sil[:, n % 2, :], ps[:, 2 * (n % 2), :], ACT.Silu).then_inc(act_sil, 1)

                def high(n):
                    act.wait_ge(dve_z, e * 4 + (n + 1 + Z0))
                    c, it = n // 2, n % 2
                    copy(z_hl[0][:, it, c * 512:(c + 1) * 512], zf[:, n % 2, :]).then_inc(act_z, 1)

                silu(0)
                for n in range(1, 4):
                    silu(n)
                    high(n - 1)
                high(3)

            with act.Fori(0, E1 + 1) as e:
                expert(e)

        @block.vector
        def _(dve):
            dve.sem_inc(dve_s, S0)
            dve.sem_inc(dve_pT, PT0)
            dve.sem_inc(dve_u, U0_)
            dve.sem_inc(dve_z, Z0)
            dve.sem_inc(dve_y, Y0)
            dve.sem_inc(dve_zl, Z0)
            dve.wait_ge(pool_const, CONSTS)
            dve.wait_ge(dma_const, 64)
            dve.sem_inc(dve_dn, DN0)

            def low(dst, src, hi):
                return dve.tensor_tensor(dst, src, raw(hi), ALU.subtract)

            def layernorm(ln):
                for q in range(QT):
                    dve.bn_stats(stats[:, q, :], xb[:, q, :]).then_inc(dve_stat, 1)
                for q in range(QT):
                    wait_alone(dve, (dve_stat, ln * QT + (q + 1)))
                    dve.bn_aggr(mv[:, q, :], stats[:, q, :]).then_inc(dve_var, 1)
                dve.wait_ge(pool_rstd, ln + 1)
                for q in range(QT):
                    dve.tensor_scalar(nat[:, q, :], xb[:, q, :], mv[:, q, 0:1], rstd[:, q:q + 1],
                                      ALU.subtract, ALU.mult).then_inc(dve_xn, 1)

            def units(u0_, layer, kk):
                def maxima(j, q, h):
                    u = u0_ + j
                    n = u * 4 + (2 * q + h + 1)
                    dve.wait_ge(pe_s, n)
                    if q == 0 and h == 0:
                        dve.wait_ge(pe_pT, u * STEPS + (PP0 - STEPS))
                    p = j % 2
                    k0_, w = HALVES[h]
                    dst = probs[:, p, q, k0_:k0_ + w]
                    if h == 1:
                        dve.wait_ge(dve_s, n - 1 + S0)
                    wait_alone(dve)
                    first = NEG if h == 0 else mx_a[:, p, q:q + 1]
                    acc = (mx_a if h == 0 else mx)[:, p, q:q + 1]
                    if layer == 0:
                        add = strided(zero, 0, (0, w))
                    else:
                        add = mask_sb[:, q, k0_:k0_ + w]
                    dve.tensor_tensor_reduce(dst, s_half(h, w), add, 1.0, first, ALU.add, ALU.max,
                                             acc).then_inc(dve_s, 1)
                    if h == 1:
                        dve.wait_ge(dve_s, n + S0)
                        dve.tensor_scalar(negmax[:, p, q:q + 1], mx[:, p, q:q + 1], -1.0, None,
                                          ALU.mult).then_inc(dve_max, 1)

                def lows(j, k):
                    u = u0_ + j
                    buf = (j + k) % 2
                    n, c = step_cols(k)
                    dve.wait_ge(act_pT, u * STEPS + (k + 1))
                    low(pT_hl[1][0:n, buf, c], ps[0:n, T[buf], c],
                        pT_hl[0][0:n, buf, c]).then_inc(dve_pT, 1)

                def head(j):
                    u = u0_ + j
                    p = j % 2
                    dve.wait_ge(act_u, u + 1)
                    dve.reciprocal(rinv[:, p, :], rowsum[:, p, :]).then_inc(dve_rinv, 1)
                    if layer == 0:
                        dve.sem_inc(dve_u, 1)
                    else:
                        low(uT_hl[1][:, p, :], ps[:, U, p * S:(p + 1) * S],
                            uT_hl[0][:, p, :]).then_inc(dve_u, 1)

                def add_out(j, q):
                    u = u0_ + j
                    dve.wait_ge(pe_y, u * QT + (q + 1))
                    if q == 0:
                        dve.wait_ge(dve_rinv, u + 1)
                    if layer == 0:
                        cols = xb[:, q, bass.ds(kk * (GRP * LKV) + j * LKV, LKV)]
                        src = ps[:, Y, 0:LKV]
                    else:
                        cols, src = xb[:, q, :], ps[:, Y, :]
                    dve.scalar_tensor_tensor(out=cols, in0=src, scalar=rinv[:, j % 2, q:q + 1], in1=cols,
                                             op0=ALU.mult, op1=ALU.add).then_inc(dve_y, 1)

                for q in range(QT):
                    for h in range(2):
                        maxima(0, q, h)
                for j in range(GRP):
                    for k in range(STEPS):
                        lows(j, k)
                        if j + 1 < GRP and k in SCORE_STEPS:
                            maxima(j + 1, *SCORE_STEPS[k])
                        if j and k in OUT_STEPS:
                            add_out(j - 1, OUT_STEPS[k])
                    head(j)
                for q in range(QT):
                    add_out(GRP - 1, q)

            link_n = [0]
            LINKS = 9

            def link(b, ins):
                link_n[0] += 1
                ins.then_inc(dve_link, 1)
                dve.wait_ge(dve_link, b * LINKS + link_n[0])

            def ranks(b, score, rank, work, n, e):
                rows, cols = (e, n), (e, n)
                per_j = strided(score, 0, (e, n), (0, e), (1, e))
                per_e = strided(score, 0, (e, n), (1, e), (0, e))
                before = strided(tri[:, 0, :], 0, (0, n), (E1, e), (1, e))
                gt, eq = [strided(w, 0, (e * e, n), (e, e), (1, e)) for w in work]
                dve.tensor_tensor(gt, per_j, per_e, ALU.is_gt).then_inc(dve_cmp, 1)
                link(b, dve.tensor_tensor(eq, per_j, per_e, ALU.is_equal))
                link(b, dve.tensor_tensor(eq, eq, before, ALU.mult))
                link(b, dve.tensor_tensor(gt, gt, eq, ALU.add))
                link(b, dve.tensor_reduce(rank, gt, AX_X, ALU.add))

            with dve.Fori(0, B) as b:
                for k in range(KT):
                    dve.wait_ge(act_ctx, b * KT + (k + 1))
                    low(ctx_hl[1][:, k, 0:NK], ctx_raw[k], ctx_hl[0][:, k, 0:NK]).then_inc(dve_ctx, 1)
                dve.wait_ge(dma_x, b * 16 + 16)
                layernorm(b * LN_PER_B)
                dve.wait_ge(pe_cq, b + 1)
                dve.tensor_copy(cqT[0:LQ, :], ps[0:LQ, Y, 0:S]).then_inc(dve_cq, 1)
                for c, (c0, n) in enumerate(CHUNKS):
                    n = min(n, NK - c0)
                    dve.wait_ge(act_k0, b * 4 + (c + 1))
                    cols = k0[P // 2:, c0:c0 + n]
                    low(cols, ps[P // 2:, c, 0:n], cols).then_inc(dve_k0, 1)
                with dve.Fori(0, BLK0) as kk:
                    blk = b * BLK0 + kk
                    for i in range(2):
                        dve.wait_ge(act_q0, blk * 2 + (i + 1))
                        for row in (LKV, 3 * LKV):
                            cols = q0[row:row + LKV, 2 * i:2 * i + 2, :]
                            dve.scalar_tensor_tensor(
                                out=cols,
                                in0=ps[row:row + LKV, T[i], :].rearrange("p (k s) -> p k s", s=S),
                                scalar=float(LKV) ** -0.5, in1=raw(cols), op0=ALU.mult,
                                op1=ALU.subtract).then_inc(dve_q0, 1)
                    units(b * UNITS + kk * GRP, 0, kk)
                dve.wait_ge(dve_y, b * (UNITS * QT) + (H0 * QT + Y0))
                layernorm(b * LN_PER_B + 1)
                link_n[0] = 0
                dve.wait_ge(pe_low, b * QT + QT)
                link(b, dve.tensor_copy(gate, ps[:, LOW[0]:LOW[0] + 2, E0 * R0:AG]))
                link(b, dve.tensor_reduce(g_m, gate, AX_X, ALU.max))
                dve.tensor_tensor(g_a, gate, strided(g_m, 0, (1, QT), (0, E0)),
                                  ALU.subtract).then_inc(dve_gate, 1)
                ranks(b, gate, g_rank, cmp0, QT, E0)
                dve.wait_ge(act_ge, b + 1)
                link(b, dve.scalar_tensor_tensor(out=g_a, in0=g_rank, scalar=2.0, in1=g_e, op0=ALU.is_lt,
                                                 op1=ALU.mult))
                link(b, dve.tensor_reduce(g_sum, g_a, AX_X, ALU.add))
                link(b, dve.reciprocal(g_m, g_sum))
                assert link_n[0] == LINKS
                dve.scalar_tensor_tensor(out=g_rank, in0=g_a, scalar=2.0,
                                         in1=strided(g_m, 0, (1, QT), (0, E0)), op0=ALU.mult,
                                         op1=ALU.mult).then_inc(dve_w, 1)
                dve.wait_ge(dve_w, b + 1)
                for q in range(QT):
                    dve.tensor_tensor(strided(lw[:, q, :], 0, (R0, E0), (1, R0)),
                                      ps[:, LOW[q], 0:P].rearrange("p (e r) -> p e r", r=R0),
                                      strided(g_rank[:, q, :], 0, (1, E0), (0, R0)),
                                      ALU.mult).then_inc(dve_lw, 1)
                for q in range(QT):
                    dve.wait_ge(pe_res, b * QT + (q + 1))
                    dve.tensor_tensor(xb[:, q, :], xb[:, q, :], ps[:, RES[q], :], ALU.add).then_inc(dve_ffn, 1)
                dve.wait_ge(dve_ffn, b * QT + QT)
                layernorm(b * LN_PER_B + 2)
                for i in range(2):
                    dve.wait_ge(act_xnT, b * (LN_PER_B * 2) + (4 + i + 1))
                    low(xnT_hl[1][:, 2 * i:2 * i + 2, :], ps[:, T[i], :].rearrange("p (k s) -> p k s", s=S),
                        xnT_hl[0][:, 2 * i:2 * i + 2, :]).then_inc(dve_xnT, 1)
                with dve.Fori(0, KVH) as g:
                    blk = b * KVH + g
                    dve.wait_ge(pool_rq, blk + 1)
                    for q in range(QT):
                        dve.tensor_tensor(nat[:, q, :].rearrange("p (h d) -> p h d", d=HD),
                                          ps[:, (Y, U)[q], :].rearrange("p (h d) -> p h d", d=HD),
                                          strided(rq, q * GRP, (1, GRP), (0, HD)),
                                          ALU.mult).then_inc(dve_qn, 1)

                    def v_low(t):
                        n = keys_in(t)
                        dve.wait_ge(act_v, blk * TT + (t + 1))
                        low(v_hl[1][0:n, t, :], ps[0:n, t % 4, P:2 * P],
                            v_hl[0][0:n, t, :]).then_inc(dve_v, 1)

                    def k_norm(t):
                        n = keys_in(t)
                        dve.wait_ge(pool_rk, blk * TT + (t + 1))
                        if t >= 4:
                            dve.wait_ge(pe_knat, blk * TT + (t - 3))
                        dve.tensor_scalar(knat[0:n, t % 4, :], ps[0:n, t % 4, 0:P], rk[0:n, t:t + 1], None,
                                          ALU.mult).then_inc(dve_kn, 1)

                    def kT(c):
                        dve.wait_ge(act_kT, blk * 4 + (c + 1))
                        n = min(512, NK - 512 * c)
                        cols = slice(512 * c, 512 * c + n)
                        dve.scalar_tensor_tensor(out=kT_hl[1][:, cols], in0=ps[:, T[c % 2], 0:n],
                                                 scalar=norm_w[:, 1:2], in1=raw(kT_hl[0][:, cols]),
                                                 op0=ALU.mult, op1=ALU.subtract).then_inc(dve_kT, 1)

                    for t in range(TT):
                        v_low(t)
                        if t:
                            k_norm(t - 1)
                        if t == Q_AT:
                            for i in range(2):
                                dve.wait_ge(act_qT, blk * 2 + (i + 1))
                                cols = qT_hl[0][:, 2 * i:2 * i + 2, :]
                                dve.scalar_tensor_tensor(
                                    out=qT_hl[1][:, 2 * i:2 * i + 2, :],
                                    in0=ps[:, T[i], :].rearrange("p (k s) -> p k s", s=S),
                                    scalar=norm_w[:, 0:1], in1=raw(cols), op0=ALU.mult,
                                    op1=ALU.subtract).then_inc(dve_qT, 1)
                        if t >= K_LAG + 3 and (t - K_LAG - 3) % 4 == 0:
                            kT((t - K_LAG - 3) // 4)
                    k_norm(TT - 1)
                    for c in range(2, 4):
                        kT(c)
                    units(b * UNITS + g * GRP + H0, 1, g)

            dve.wait_ge(dma_xall, 16)
            for t in range(TOK):
                dve.bn_stats(stats[:, t, :], x_all[:, t, :]).then_inc(dve_stat, 1)
            for t in range(TOK):
                dve.wait_ge(dve_stat, B * LN_PER_B * QT + (t + 1))
                dve.bn_aggr(mv[:, t, :], stats[:, t, :]).then_inc(dve_var, 1)
            dve.wait_ge(pool_rstd, B * LN_PER_B + 1)

            def x_low(t):
                dve.wait_ge(act_xg, t + 1)
                cols = xnT_all[0][:, :, t * P:(t + 1) * P]
                low(xnT_all[1][:, :, t * P:(t + 1) * P],
                    ps[:, T[t % 2], :].rearrange("p (k s) -> p k s", s=P), cols).then_inc(dve_xlo, 1)

            for t in range(TOK):
                if t >= 2:
                    dve.wait_ge(pe_mx, t - 1)
                dve.tensor_scalar(xnat[t % 2], x_all[:, t, :], mv[:, t, 0:1], rstd[:, t:t + 1],
                                  ALU.subtract, ALU.mult).then_inc(dve_xnat, 1)
                if t:
                    x_low(t - 1)
            x_low(TOK - 1)
            link_n[0] = 0
            b = B
            dve.wait_ge(act_lg, 1)
            dve.wait_ge(dma_gate, 32)
            dve.memset(cw, 1.0).then_inc(dve_cmp, 1)
            link(b, dve.tensor_tensor(sc, sc, strided(bias_sb, 0, (0, TOK), (1, E1)), ALU.add))
            ranks(b, sc, rank, cmp1, TOK, E1)
            link(b, dve.scalar_tensor_tensor(out=rank, in0=rank, scalar=float(TOPK), in1=sc, op0=ALU.is_lt,
                                             op1=ALU.mult))
            link(b, dve.tensor_reduce(wsum, rank, AX_X, ALU.add))
            link(b, dve.tensor_scalar(wsum, wsum, 1e-20, None, ALU.add))
            link(b, dve.reciprocal(wsum, wsum))
            dve.tensor_tensor(cw[:, :, 0:E1], rank, strided(wsum, 0, (1, TOK), (0, E1)),
                              ALU.mult).then_inc(dve_cw, 1)
            dve.wait_ge(dve_cw, 1)

            def expert(e):
                def product(n):
                    dve.wait_ge(act_sil, e * 4 + (n + 1))
                    dve.wait_ge(dve_zl, e * 4 + (n + 1 - 2 + Z0))
                    dve.wait_ge(act_z, e * 4 + (n + 1 - 2 + Z0))
                    dve.tensor_tensor(zf[:, n % 2, :], sil[:, n % 2, :], ps[:, 2 * (n % 2) + 1, :],
                                      ALU.mult).then_inc(dve_z, 1)

                def z_low(n):
                    dve.wait_ge(act_z, e * 4 + (n + 1 + Z0))
                    c, it = n // 2, n % 2
                    cols = slice(c * 512, (c + 1) * 512)
                    low(z_hl[1][:, it, cols], zf[:, n % 2, :], z_hl[0][:, it, cols]).then_inc(dve_zl, 1)

                product(0)
                for n in range(1, 4):
                    product(n)
                    z_low(n - 1)
                z_low(3)
                for t in range(TOK):
                    dve.wait_ge(pe_dn, e * TOK + (t + 1))
                    dve.scalar_tensor_tensor(out=x_all[:, t, :], in0=ps[:, 4 + t % 4, :],
                                             scalar=cw[:, t, bass.ds(e, 1)], in1=x_all[:, t, :],
                                             op0=ALU.mult, op1=ALU.add).then_inc(dve_dn, 1)

            with dve.Fori(0, E1 + 1) as e:
                expert(e)


def kernel(**inputs):
    import numpy as np
    import concourse.bacc as bacc
    from concourse.bass_utils import run_bass_kernel_spmd as run

    a = {k: np.asarray(v) for k, v in inputs.items()}

    def rows(w, n):
        r = w.reshape(w.shape[:-2] + (w.shape[-2] // P, P, n))
        return np.swapaxes(r, -3, -2)

    def ahead(w):
        return np.concatenate([w, w[:1]], axis=0)

    wqk = a["L0_xattn_W_qk"].reshape(LQ, BLK0, GRP, 1, LKV)
    wqk = np.broadcast_to(wqk, (LQ, BLK0, GRP, 4, LKV)).reshape(LQ, BLK0, GRP, P).transpose(1, 0, 2, 3)
    wdkv = np.broadcast_to(a["L0_xattn_Wkv_d"][:, None, :], (D, 4, LKV)).reshape(D, P)
    wvu = np.zeros((4, LKV, H0 * LKV), np.float32)
    wvu[0] = wvu[2] = a["L0_xattn_Wv_u"]
    ag = np.concatenate([a["L0_ffn_lora_A"].reshape(E0 * R0, D), a["L0_ffn_gate_w"]], axis=0).T
    wq = a["L1_xattn_Wq"].reshape(KVH, 2, 2 * HD, D).transpose(0, 1, 3, 2)
    wo = a["L1_xattn_Wo"].T.reshape(KVH, 2, 2, HD, D).transpose(0, 1, 3, 2, 4)
    wg = np.concatenate([a["L1_ffn_Wg"], a["L1_ffn_Sg"][None]], axis=0).transpose(0, 2, 1)
    wu = np.concatenate([a["L1_ffn_Wu"], a["L1_ffn_Su"][None]], axis=0).transpose(0, 2, 1)
    wd = np.concatenate([a["L1_ffn_Wd"], a["L1_ffn_Sd"][None]], axis=0).transpose(0, 2, 1)
    laid = {
        "x": a["x"].reshape(B, QT, P, D),
        "ctx_t": a["ctx_4096"].transpose(0, 2, 1).reshape(B, KT, P, NK),
        "mask": a["mask_1x1xSxS2_ff0"].reshape(QT, P, NK),
        "wqd": rows(a["L0_xattn_Wq_d"], LQ),
        "wqk": wqk,
        "wdkv": rows(wdkv, P),
        "wvu": wvu.reshape(P, H0 * LKV),
        "ag_t": rows(ag, AG),
        "base_t": rows(a["L0_ffn_base_w"].T, D),
        "base_b": a["L0_ffn_base_b"].reshape(1, D),
        "lora_b": a["L0_ffn_lora_B"].transpose(0, 2, 1).reshape(E0 * R0, D),
        "wk": ahead(rows(a["L1_xattn_Wk"].reshape(KVH, HD, D).transpose(0, 2, 1), HD)),
        "wv": ahead(rows(a["L1_xattn_Wv"].reshape(KVH, HD, D).transpose(0, 2, 1), HD)),
        "wq": ahead(rows(wq, 2 * HD).reshape(KVH, 2, P, KT * 2 * HD)),
        "wo": wo.reshape(KVH, 2, P, 2 * D),
        "norms": np.stack([a["L1_xattn_q_norm_w"], a["L1_xattn_k_norm_w"]], axis=1),
        "gate_t": rows(a["L1_ffn_gate_w"].T, E1),
        "gate_bias": np.broadcast_to(a["L1_ffn_bias"], (P, E1)),
        "wg": rows(wg, INNER).reshape(E1 + 1, P, KT * INNER),
        "wu": rows(wu, INNER).reshape(E1 + 1, P, KT * INNER),
        "wd": rows(wd, D).reshape(E1 + 1, P, 2 * D),
    }
    nc = bacc.Bacc("TRN2", target_bir_lowering=False, num_devices=1)
    arrays, args = {}, {}
    for name, v in laid.items():
        v = np.ascontiguousarray(v)
        arrays[f"in_{name}"] = v
        args[name] = nc.dram_tensor(f"in_{name}", v.shape, mybir.dt.from_np(v.dtype),
                                    kind="ExternalInput").ap()
    args["out"] = nc.dram_tensor("out_x", (B, QT, P, D), F32, kind="ExternalOutput").ap()
    args["x_mid"] = nc.dram_tensor("x_mid", (B, QT, P, D), F32, kind="Internal").ap()
    xattn_ffn_kernel(nc, **args)
    r = run(nc, [arrays], core_ids=[0])
    return np.asarray(r.results[0]["out_x"]).reshape(B, S, D)
```

```python
from contextlib import ExitStack

import concourse.bass as bass
from concourse import mybir

F32 = mybir.dt.float32
F32R = mybir.dt.float32r
ALU = mybir.AluOpType
ACT = mybir.ActivationFunctionType
AX_X = mybir.AxisListType.X

P = 128
B, S, D = 4, 256, 512
NK = 1601
NKP = NK + 1
KT = D // P
QT = S // P
TT = -(-NK // P)
LAST = NK - (TT - 1) * P
STEPS = -(-TT // 2)
H0, LQ, LKV = 16, 64, 32
E0, R0 = 8, 16
KVH, GRP, HD = 8, 4, 128
E1, INNER, TOPK = 16, 256, 4
TOK = B * S // P
BLK0 = H0 // GRP
BLKS = BLK0 + KVH
UNITS = BLKS * GRP
EPS = 1e-5
NEG = -3.0e38
CHUNKS = [(0, 512), (512, 288), (800, 512), (1312, 290)]
HALVES = [(0, 800), (800, 801)]
AG = E0 * R0 + E0


def keys_in(t):
    return P if t < TT - 1 else LAST


def xattn_ffn_kernel(nc, x, ctx_t, mask, wqd, wqk, wdkv, wvu, ag_t, base_t, base_b, lora_b, wk, wv, wq, wo,
                     norms, gate_t, gate_bias, wg, wu, wd, out, x_mid):
    with ExitStack() as ctx:
        def sem(name):
            return ctx.enter_context(nc.semaphore(name))

        R_COLS, F_COLS = 36756, 16434
        arena_r = ctx.enter_context(nc.sbuf_tensor("arena_r", [P, R_COLS], F32R))
        arena_f = ctx.enter_context(nc.sbuf_tensor("arena_f", [P, F_COLS], F32))
        ps = ctx.enter_context(nc.psum_tensor("ps", [P, 8, 512], F32))
        top = {"r": 0, "f": 0}

        def take(which, *dims, at=None):
            n = 1
            for d in dims:
                n *= d
            arena = arena_r if which == "r" else arena_f
            if at is None:
                at = top[which]
                top[which] += n
            assert at + n <= (R_COLS if which == "r" else F_COLS), (which, at + n)
            v = arena[:, at:at + n]
            if len(dims) == 2:
                v = v.rearrange("p (a b) -> p a b", b=dims[1])
            if len(dims) == 3:
                v = v.rearrange("p (a b c) -> p a b c", b=dims[1], c=dims[2])
            return v

        def raw(v):
            return v.bitcast(F32)

        ctx_hl = [take("r", KT, NKP) for _ in range(2)]
        wkv_hl = [take("r", 2, KT, HD) for _ in range(2)]
        wq_hl = [take("r", 2, KT, 2 * HD) for _ in range(2)]
        wo_hl = [take("r", 2, D) for _ in range(2)]
        kT_hl = [take("r", NKP) for _ in range(2)]
        v_hl = [take("r", TT, P) for _ in range(2)]
        xnT_hl = [take("r", KT, S) for _ in range(2)]
        qT_hl = [take("r", GRP, S) for _ in range(2)]
        pT_hl = [take("r", 3, 512) for _ in range(2)]
        uT_hl = [take("r", 2, S) for _ in range(2)]
        wdkv_hl = [take("r", KT, P) for _ in range(2)]
        k0 = kT_hl[0]
        v0 = v_hl[0]
        q0 = qT_hl[0]

        p_at = top["f"]
        probs = take("f", 2, QT, NKP)
        ctx_raw = [take("f", NK, at=p_at + i * NKP) for i in range(KT)]
        base_sb = take("f", KT, D, at=p_at)
        ag_sb = take("f", KT, AG, at=p_at + 2048)
        lorab_sb = take("f", D, at=p_at + 2592)
        baseb_sb = take("f", D, at=p_at + 3104)
        lw = take("f", QT, P, at=p_at + 3616)
        lwT = take("f", QT, P, at=p_at + 3872)
        cmp0 = [take("f", QT * E0 * E0, at=p_at + 4128 + i * QT * E0 * E0) for i in range(2)]
        xnT_f = take("f", KT, S, at=p_at + 4 * NKP - KT * S)
        mask_sb = take("f", QT, NK)
        xb = take("f", QT, D)
        nat = take("f", QT, D)
        raw_at = top["f"]
        raw_w = take("f", 2, 1024)
        knat = take("f", 4, P)
        u0 = take("f", 2, S, at=top["f"] - 512)
        cqT = take("f", S)
        wvu_sb = take("f", D)
        wqk_sb = take("f", GRP, P, at=raw_at)
        wqd_sb = take("f", KT, LQ, at=raw_at + GRP * P)
        const_at = top["f"]
        ident = take("f", P)
        ones = take("f", P)
        junk = take("f", 2, P)
        norm_w = take("f", 2)
        half_exp = take("f", TOK)
        zero = take("f", 1)
        tri = take("f", E1, E1)
        ssq = take("f", TT)
        mid = take("f", TOK)
        rk = take("f", TT)
        qss = take("f", QT * GRP)
        rq = take("f", QT * GRP)
        mx = take("f", 2, QT)
        mx_a = take("f", 2, QT)
        negmax = take("f", 2, QT)
        rowsum = take("f", GRP, QT)
        rinv = take("f", 2, QT)
        stats = take("f", TOK, 6)
        mv = take("f", TOK, 2)
        rstd = take("f", TOK)
        gate = take("f", QT, E0)
        g_e = take("f", QT, E0)
        g_rank = take("f", QT, E0)
        g_a = take("f", QT, E0)
        g_m = take("f", QT)
        g_sum = take("f", QT)

        def s_half(h, n):
            return ps[:, 2 * h:2 * h + 2, :].rearrange("p a b -> p (a b)")[:, 0:n]

        def strided(view, off, *dims):
            a = view[:, off:off + 1]
            return bass.AP(tensor=a.tensor, offset=a.offset, ap=[list(a.ap[0])] + [list(d) for d in dims])

        def step_cols(k):
            return (P, slice(0, 512)) if k < STEPS - 1 else (LAST, slice(0, S))

        LOW, RES, TRN = (0, 1), (2, 3), (6, 7)
        QUARTERS = [(0, 0), (0, 1), (1, 0), (1, 1)]
        SCORE_AT = [(-3, -2, -1, 0), (-3, -2, 0, 1)]
        MAX_AT = [(-2, -1, 0, 1), (-2, -1, 1, 2)]
        EXP_AT = [(1, 4), (1, 4)]
        OUT_STEPS = {2: 0, 5: 1}
        ADD_STEPS = {3: 0, 6: 1}
        Q1_STEPS = {21: (0, 0), 22: (0, 1), 24: (1, 0), 25: (1, 1)}
        SQUARE_STEPS = {23: 0, 26: 1}
        KV_EARLY = 2
        KV_BANKS = (2, 3, 0, 1, 6, 7, 2, 3, 6, 7, 2, 3, 6)
        assert len(KV_BANKS) == TT
        FIRST_HALVES = [(0, 0), (1, 0)]
        Q0_STEPS = {14: 0, 15: 1}
        AHEAD = 2
        BLOCK_STEPS = GRP * STEPS
        Q_AT, K_LAG = 1, 3

        T, Y, U = (4, 5), 6, 7
        RING = (4, 5, 6)

        class Plan:

            def __init__(self, layer, cont, more):
                self.layer, self.cont, self.more = layer, cont, more
                self.first_out = -1 if cont else 0
                cycle = []
                for s in range(BLOCK_STEPS):
                    cycle.append(("T", s + AHEAD))
                    if layer == 0 and s in Q0_STEPS:
                        cycle.append(("Q", Q0_STEPS[s]))
                    if s % STEPS in OUT_STEPS:
                        cycle.append(("Y", (s // STEPS - 1) * QT + OUT_STEPS[s % STEPS]))
                if layer == 0:
                    cycle += [None] * (-len(cycle) % len(RING))
                else:
                    cycle = [use for use in cycle if self.exists(use)] + [None] * QT
                self.cycle = cycle
                self.at = {use: p for p, use in enumerate(cycle)}
                if not more:
                    for q in range(QT):
                        self.at[("Y", (GRP - 1) * QT + q)] = len(cycle) - QT + q
                for i in range(AHEAD):
                    self.at[("T", i)] = self.at.get(("T", BLOCK_STEPS + i), len(cycle) - AHEAD + i) - len(cycle)

            def exists(self, use):
                return use is not None and {
                    "T": use[1] < BLOCK_STEPS or self.more,
                    "Y": use[1] >= 0 or self.cont,
                    "Q": self.more}[use[0]]

            def bank(self, use):
                return RING[self.at[use] % len(RING)]

            def before(self, use):
                p = self.at[use] - len(RING)
                while p >= -len(self.cycle):
                    last = self.cycle[p]
                    if p < 0 and self.layer == 1:
                        i = p + AHEAD
                        return ("T", i) if i >= 0 else None
                    if p >= 0 and self.exists(last):
                        return last
                    if p < 0 and last is not None and last[0] == "T" and last[1] >= BLOCK_STEPS:
                        return ("T", last[1] - BLOCK_STEPS)
                    if p < 0 and last is not None and self.cont:
                        return (last[0], last[1] - {"T": BLOCK_STEPS, "Y": GRP * QT, "Q": 2}[last[0]])
                    p -= len(RING)
                return None

            def order(self, j):
                if self.layer == 1 and j == 0:
                    return FIRST_HALVES + [(0, 1), (1, 1)]
                return QUARTERS

            def first_scores(self):
                return [] if self.cont else self.order(0)[2 if self.layer == 1 else 0:]

            def others(self, s, places):
                for j in range(1, GRP + 2):
                    for i, place in enumerate(places[self.layer]):
                        at = (j - 1) * STEPS + place
                        if j >= GRP and not self.more:
                            continue
                        if at == s if s >= 0 else (at < 0 and not self.cont):
                            yield j, i

            def outs(self, s, steps):
                if s % STEPS in steps and s // STEPS - 1 >= self.first_out:
                    yield s // STEPS - 1, steps[s % STEPS]

            def heads_done(self, s):
                if s % STEPS == 0 and s // STEPS - 1 >= self.first_out:
                    yield s // STEPS - 1

        def batches(eng, run):
            with eng.Fori(0, B - 1) as b:
                run(b, True)
            run(B - 1, False)

        def layer1_blocks(eng, run):
            plan = Plan(1, False, False)
            with eng.Fori(0, KVH - 1) as g:
                run(g, plan, True)
            run(KVH - 1, plan, False)

        def layer0_blocks(eng, run):
            run(0, Plan(0, False, True))
            with eng.Fori(1, BLK0 - 1) as k:
                run(k, Plan(0, True, True))
            run(BLK0 - 1, Plan(0, True, False))

        dma_const = sem("dma_const")
        dma_ctx = [sem(f"dma_ctx{i}") for i in range(KT)]
        dma_x = sem("dma_x")
        dma_x_out = sem("dma_x_out")
        dma_wqd = sem("dma_wqd")
        dma_wqk = sem("dma_wqk")
        dma_ffn = sem("dma_ffn")
        dma_raw = [sem(f"dma_raw{i}") for i in range(2)]
        dma_out = sem("dma_out")
        pool_const = sem("pool_const")
        pool_split = sem("pool_split")
        pool_tmp = sem("pool_tmp")
        pool_rstd = sem("pool_rstd")
        pool_rq = sem("pool_rq")
        pool_rk = sem("pool_rk")
        act_ctx = sem("act_ctx")
        dve_ctx = sem("dve_ctx")
        dve_stat = sem("dve_stat")
        dve_var = sem("dve_var")
        dve_xn = sem("dve_xn")
        pe_xn = sem("pe_xn")
        act_xnT = sem("act_xnT")
        dve_xnT = sem("dve_xnT")
        pe_cq = sem("pe_cq")
        dve_cq = sem("dve_cq")
        pe_k0 = sem("pe_k0")
        act_k0 = sem("act_k0")
        dve_k0 = sem("dve_k0")
        pe_v0 = sem("pe_v0")
        act_v0 = sem("act_v0")
        pe_q0 = sem("pe_q0")
        act_q0 = sem("act_q0")
        dve_q0 = sem("dve_q0")
        pe_q = sem("pe_q")
        act_qss = sem("act_qss")
        dve_qn = sem("dve_qn")
        pe_qT = sem("pe_qT")
        act_qT = sem("act_qT")
        dve_qT = sem("dve_qT")
        pe_kv = sem("pe_kv")
        act_kss = sem("act_kss")
        act_v = sem("act_v")
        dve_v = sem("dve_v")
        dve_kn = sem("dve_kn")
        pe_knat = sem("pe_knat")
        act_kT = sem("act_kT")
        dve_kT = sem("dve_kT")
        pe_s = sem("pe_s")
        dve_s = sem("dve_s")
        dve_max = sem("dve_max")
        act_p = sem("act_p")
        pe_pT = sem("pe_pT")
        act_pT = sem("act_pT")
        dve_pT = sem("dve_pT")
        pe_av = sem("pe_av")
        act_u = sem("act_u")
        dve_u = sem("dve_u")
        dve_rinv = sem("dve_rinv")
        pe_y = sem("pe_y")
        dve_y = sem("dve_y")
        pe_low = sem("pe_low")
        pe_res = sem("pe_res")
        act_ge = sem("act_ge")
        dve_gate = sem("dve_gate")
        dve_lw = sem("dve_lw")
        pe_lw = sem("pe_lw")
        act_lw = sem("act_lw")
        dve_ffn = sem("dve_ffn")
        dve_link = sem("dve_link")
        dve_cmp = sem("dve_cmp")
        dve_w = sem("dve_w")
        pool_wo = sem("pool_wo")
        alone = {e.engine: sem(f"alone_{n}") for n, e in (("pe", nc.tensor), ("dve", nc.vector),
                                                          ("pool", nc.gpsimd))}
        dma_xall = [sem(f"dma_xall{i}") for i in range(B)]
        dma_gate = sem("dma_gate")
        dve_xnat = sem("dve_xnat")
        pe_mx = sem("pe_mx")
        act_xhi = sem("act_xhi")
        act_xg = sem("act_xg")
        dve_xlo = sem("dve_xlo")
        pe_lg = sem("pe_lg")
        act_lg = sem("act_lg")
        dve_cw = sem("dve_cw")
        pe_gu = sem("pe_gu")
        act_sil = sem("act_sil")
        dve_z = sem("dve_z")
        act_z = sem("act_z")
        dve_zl = sem("dve_zl")
        pe_dn = sem("pe_dn")
        dve_dn = sem("dve_dn")

        S0, PT0, PP0, AV0, U0_, Z0, DN0, Y0, Q0, X0, KV0 = 2, 2, STEPS + 1, 3, 2, 2, 4, 1, 1, 16, 1
        LN_PER_B = 3
        SPLIT0, SPLITB = 5, 6

        xnT_all = [take("r", KT, TOK * P, at=i * KT * TOK * P) for i in range(2)]
        er_at = 2 * KT * TOK * P
        E_R = 2 * KT * INNER + 2 * D
        ew = [[take("r", E_R, at=er_at + (2 * b + i) * E_R) for i in range(2)] for b in range(2)]
        z_hl = [take("r", 2, TOK * P, at=er_at + 4 * E_R + i * 2 * TOK * P) for i in range(2)]

        def gu_w(buf, part, which):
            return ew[buf][part][:, which * KT * INNER:(which + 1) * KT * INNER].rearrange(
                "p (k i) -> p k i", i=INNER)

        def dn_w(buf, part):
            return ew[buf][part][:, 2 * KT * INNER:].rearrange("p (k n) -> p k n", n=D)

        x_all = take("f", TOK, D, at=0)
        raw_e = [take("f", E_R, at=TOK * D + i * E_R) for i in range(2)]
        m_at = TOK * D + 2 * E_R
        sil = take("f", 2, 512, at=m_at)
        zf = take("f", 2, 512, at=m_at + 1024)
        xnat = [take("f", D, at=m_at + i * D) for i in range(2)]
        xnT_g = [take("f", KT, P, at=m_at + 1024 + i * 512) for i in range(2)]
        gate_sb = take("f", KT, E1, at=m_at + 2048)
        bias_sb = take("f", E1, at=m_at + 2112)
        sc = take("f", TOK, E1, at=m_at + 2128)
        cw = take("f", TOK, E1 + 1, at=m_at + 2256)
        rank = take("f", TOK, E1, at=m_at + 2400)
        wsum = take("f", TOK, at=m_at + 2528)
        cmp1 = [take("f", TOK * E1 * E1, at=m_at), take("f", TOK * E1 * E1, at=m_at + 2540)]
        assert m_at + 2540 + TOK * E1 * E1 <= const_at

        CONSTS = 11

        def wait_alone(eng, *waits):
            for s_, value in waits:
                eng.wait_ge(s_, value)
            eng.sem_inc(alone[eng.engine], 1)

        block = ctx.enter_context(nc.Block())

        @block.sync
        def _(sp):
            sp.sem_inc(dma_x_out, X0)
            def load(n, slot, dst, src):
                sp.wait_ge(pool_split, n - 1)
                sp.dma_start(dst, src).then_inc(dma_raw[slot], 16)

            def kv_part(slot):
                return raw_w[:, slot, 0:KT * HD].rearrange("p (k d) -> p k d", d=HD)

            def load_ctx(b):
                for k in range(KT):
                    sp.dma_start(ctx_raw[k], ctx_t[b, k]).then_inc(dma_ctx[k], 16)

            sp.dma_start(kv_part(0), wdkv).then_inc(dma_raw[0], 16)
            sp.dma_start(kv_part(1), wk[0]).then_inc(dma_raw[1], 16)
            load_ctx(0)
            load(2, 0, kv_part(0), wv[0])
            load(3, 1, raw_w[:, 1, :], wq[0, 0])
            load(4, 0, raw_w[:, 0, :], wq[0, 1])
            for dst, src in ((wvu_sb, wvu), (norm_w, norms), (mask_sb, mask.rearrange("t p k -> p t k"))):
                sp.dma_start(dst, src).then_inc(dma_const, 16)

            def batch(b, more):
                sp.wait_ge(dma_x_out, b * 16 + X0)
                sp.dma_start(xb, x[b].rearrange("t p d -> p t d")).then_inc(dma_x, 16)
                sp.wait_ge(pool_split, b * (KVH * SPLITB) + SPLIT0)
                sp.dma_start(wqd_sb, wqd).then_inc(dma_wqd, 16)
                with sp.Fori(0, BLK0) as k:
                    sp.wait_ge(pe_q0, (b * BLK0 + k) * 2 + Q0)
                    sp.dma_start(wqk_sb[0:LQ], wqk[k]).then_inc(dma_wqk, 16)
                sp.wait_ge(pe_pT, b * (UNITS * STEPS) + H0 * STEPS + PP0)
                for dst, src in ((base_sb, base_t), (ag_sb, ag_t), (lorab_sb, lora_b),
                                 (baseb_sb[0:1], base_b)):
                    sp.dma_start(dst, src).then_inc(dma_ffn, 16)
                with sp.Fori(0, KVH) as g:
                    n = b * (KVH * SPLITB) + g * SPLITB + SPLIT0
                    load(n, 1, raw_w[:, 1, :], wo[g, 0])
                    load(n + 1, 0, kv_part(0), wk[g + 1])
                    load(n + 2, 1, kv_part(1), wv[g + 1])
                    load(n + 3, 0, raw_w[:, 0, :], wq[g + 1, 0])
                    load(n + 4, 1, raw_w[:, 1, :], wq[g + 1, 1])
                    load(n + 5, 0, raw_w[:, 0, :], wo[g, 1])
                if more:
                    sp.wait_ge(pe_pT, (b + 1) * (UNITS * STEPS) + PP0)
                    load_ctx(b + 1)

            batches(sp, batch)
            assert (B - 1) * QT * D <= QT * NKP
            sp.wait_ge(pe_pT, (B * UNITS - 1) * STEPS + PP0)
            for b in range(B):
                if b == B - 1:
                    sp.wait_ge(dma_x_out, B * 16 + X0)
                    sp.wait_ge(pe_y, B * UNITS * QT)
                sp.dma_start(x_all[:, b * QT:(b + 1) * QT, :],
                             x_mid[b].rearrange("t p d -> p t d")).then_inc(dma_xall[b], 16)
            sp.wait_ge(pool_split, B * KVH * SPLITB + SPLIT0)
            sp.dma_start(gate_sb, gate_t).then_inc(dma_gate, 16)
            sp.dma_start(bias_sb, gate_bias).then_inc(dma_gate, 16)
            base = B * KVH * SPLITB + SPLIT0

            def load_expert(e, slot):
                n = KT * INNER
                sp.dma_start(raw_e[slot][:, 0:n], wg[e]).then_inc(dma_raw[slot], 16)
                sp.dma_start(raw_e[slot][:, n:2 * n], wu[e]).then_inc(dma_raw[slot], 16)
                sp.dma_start(raw_e[slot][:, 2 * n:], wd[e]).then_inc(dma_raw[slot], 16)

            load_expert(0, 0)
            load_expert(1, 1)
            with sp.Fori(0, E1 // 2 - 1) as i:
                for j in range(2):
                    sp.wait_ge(pool_split, i * 2 + (base + 1 + j))
                    load_expert(i * 2 + (2 + j), j)
            sp.wait_ge(pool_split, base + E1 - 1)
            load_expert(E1, 0)
            sp.wait_ge(dve_dn, (E1 + 1) * TOK + DN0)
            sp.dma_start(out.rearrange("b t p d -> p b t d"),
                         x_all.rearrange("p (b t) d -> p b t d", t=QT)).then_inc(dma_out, 16)
            sp.wait_ge(dma_out, 16)

        @block.gpsimd
        def _(pool):
            def step(ins):
                ins.then_inc(pool_const, 1)

            step(pool.memset(ident, 0.0))
            step(pool.memset(ones, 1.0))
            step(pool.memset(half_exp, -0.5))
            step(pool.memset(tri, 1.0))
            step(pool.memset(zero, 0.0))
            step(pool.memset(raw(ctx_hl[0][:, :, NK:NKP]), 0.0))
            step(pool.memset(raw(ctx_hl[1][:, :, NK:NKP]), 0.0))
            step(pool.memset(raw(kT_hl[0][:, NK:NKP]), 0.0))
            step(pool.memset(raw(kT_hl[1][:, NK:NKP]), 0.0))
            pool.wait_ge(pool_const, CONSTS - 2)
            step(pool.affine_select(out=ident, in_=ident, compare_op=ALU.not_equal, fill=1.0, base=0,
                                    pattern=[[-1, P]], channel_multiplier=1))
            step(pool.affine_select(out=tri, in_=tri, compare_op=ALU.is_gt, fill=0.0, base=0,
                                    pattern=[[1, E1], [-1, E1]], channel_multiplier=0))

            pool.wait_ge(pool_const, CONSTS)

            def kv_raw(slot):
                return raw_w[:, slot, 0:KT * HD].rearrange("p (k d) -> p k d", d=HD)

            def q_raw(slot):
                return raw_w[:, slot, :].rearrange("p (k d) -> p k d", d=2 * HD)

            def split_chunk(slot, loads, dsts, src, hi_n):
                pool.wait_ge(dma_raw[slot], loads)
                wait_alone(pool)
                pool.tensor_copy(dsts[0], src).then_inc(pool_tmp, 1)
                pool.wait_ge(pool_tmp, hi_n)
                return pool.tensor_tensor(dsts[1], src, raw(dsts[0]), ALU.subtract)

            def pick(hl, *idx):
                return [hl[0][idx], hl[1][idx]]

            every = slice(None)
            split_chunk(0, 16, wdkv_hl, kv_raw(0), 1).then_inc(pool_split, 1)
            split_chunk(1, 16, pick(wkv_hl, every, 0), kv_raw(1), 2).then_inc(pool_split, 1)
            split_chunk(0, 32, pick(wkv_hl, every, 1), kv_raw(0), 3).then_inc(pool_split, 1)
            split_chunk(1, 32, pick(wq_hl, every, 0), q_raw(1), 4).then_inc(pool_split, 1)
            split_chunk(0, 48, pick(wq_hl, every, 1), q_raw(0), 5).then_inc(pool_split, 1)

            TMP_BLK = 1 + TT + SPLITB + 2
            TMP_B = LN_PER_B + KVH * TMP_BLK

            def inverse_root(dst, src, mul, add, tmp_n):
                wait_alone(pool)
                n = dst.shape[-1]
                pool.tensor_scalar(mid[:, 0:n], src, mul, add, ALU.mult, ALU.add).then_inc(pool_tmp, 1)
                pool.wait_ge(pool_tmp, tmp_n)
                return pool.tensor_tensor(dst, mid[:, 0:n], half_exp[:, 0:n], ALU.pow)

            def batch(b, more):
                for ln in range(LN_PER_B):
                    tmp_n = b * TMP_B + (5 + ln + 1)
                    pool.wait_ge(dve_var, b * (LN_PER_B * QT) + (ln + 1) * QT)
                    inverse_root(rstd[:, 0:QT], mv[:, 0:QT, 1], 1.0, EPS, tmp_n).then_inc(pool_rstd, 1)
                    pool.wait_ge(pool_rstd, b * LN_PER_B + (ln + 1))
                wait_alone(pool)
                with pool.Fori(0, KVH) as g:
                    blk = b * KVH + g
                    t0 = b * TMP_B + g * TMP_BLK + (5 + LN_PER_B)
                    pool.wait_ge(act_qss, blk * (QT * GRP) + QT * GRP)
                    inverse_root(rq, qss, 1.0, HD * EPS, t0 + 1).then_inc(pool_rq, 1)
                    pool.wait_ge(pool_rq, blk + 1)
                    for t in range(TT):
                        n = keys_in(t)
                        wait_alone(pool, (act_kss, blk * TT + (t + 1)))
                        pool.tensor_scalar(mid[0:n, 0:1], ssq[0:n, t:t + 1], 1.0 / HD, EPS, ALU.mult,
                                           ALU.add).then_inc(pool_tmp, 1)
                        pool.wait_ge(pool_tmp, t0 + (t + 2))
                        pool.tensor_tensor(rk[0:n, t:t + 1], mid[0:n, 0:1], half_exp[0:n, 0:1],
                                           ALU.pow).then_inc(pool_rk, 1)
                        pool.wait_ge(pool_rk, blk * TT + (t + 1))
                    ld = blk * (3 * 16)
                    m = t0 + (1 + TT)

                    def split_o(pair, slot, loads, m):
                        for i in range(2):
                            j = 2 * pair + i
                            head = b * UNITS + g * GRP + (H0 + j)
                            pool.wait_ge(pe_y, head * QT - QT)
                            ins = split_chunk(slot, loads, pick(wo_hl, every, i),
                                              raw_w[:, slot, i * D:(i + 1) * D], m + (i + 1))
                            ins.then_inc(pool_wo, 1)
                        return ins

                    split_o(0, 1, ld + 48, m)
                    pool.wait_ge(pool_wo, blk * GRP + 2)
                    pool.sem_inc(pool_split, 1)
                    pool.wait_ge(pe_kv, blk * TT + (TT + KV0))
                    split_chunk(0, ld + 64, pick(wkv_hl, every, 0), kv_raw(0), m + 3).then_inc(pool_split, 1)
                    split_chunk(1, ld + 64, pick(wkv_hl, every, 1), kv_raw(1), m + 4).then_inc(pool_split, 1)
                    split_chunk(0, ld + 80, pick(wq_hl, every, 0), q_raw(0), m + 5).then_inc(pool_split, 1)
                    split_chunk(1, ld + 80, pick(wq_hl, every, 1), q_raw(1), m + 6).then_inc(pool_split, 1)
                    split_o(1, 0, ld + 96, m + 6)
                    pool.wait_ge(pool_wo, blk * GRP + 4)
                    pool.sem_inc(pool_split, 1)

            batches(pool, batch)

            t1 = 5 + B * TMP_B
            pool.wait_ge(dve_var, B * LN_PER_B * QT + TOK)
            inverse_root(rstd, mv[:, :, 1], 1.0, EPS, t1 + 1).then_inc(pool_rstd, 1)
            pool.wait_ge(pe_y, B * UNITS * QT)

            def split_expert(e, slot, loads, tmp_n):
                pool.wait_ge(dma_raw[slot], loads)
                wait_alone(pool)
                pool.tensor_copy(ew[slot][0], raw_e[slot]).then_inc(pool_tmp, 1)
                pool.wait_ge(pool_tmp, tmp_n)
                pool.tensor_tensor(ew[slot][1], raw_e[slot], raw(ew[slot][0]),
                                   ALU.subtract).then_inc(pool_split, 1)

            had = [16 * (3 + 3 * B * KVH), 16 * (2 + 3 * B * KVH)]
            for e in range(2):
                split_expert(e, e, had[e] + 48, t1 + 2 + e)
            with pool.Fori(0, E1 // 2 - 1) as i:
                for j in range(2):
                    pool.wait_ge(pe_dn, i * (2 * TOK) + (j + 1) * TOK)
                    split_expert(None, j, i * 48 + (had[j] + 96), i * 2 + (t1 + 4 + j))
            pool.wait_ge(pe_dn, (E1 - 1) * TOK)
            split_expert(None, 0, had[0] + 48 * 9, t1 + 2 + E1)

        def unit_mm(pe, dst, left, right, parts, start, stop):
            for n, (a, c) in enumerate(parts):
                ins = pe.matmul(dst, left[a], right[c], start=start and n == 0,
                                stop=stop and n == len(parts) - 1)
            return ins

        THREE = ((0, 0), (0, 1), (1, 0))

        @block.tensor
        def _(pe):
            pe.sem_inc(pe_pT, PP0)
            pe.sem_inc(pe_av, AV0)
            pe.sem_inc(pe_q0, Q0)
            pe.sem_inc(pe_kv, KV0)
            pe.wait_ge(pool_const, CONSTS)

            def transpose_x(ln):
                pe.wait_ge(dve_xn, ln * QT + QT)
                for k in range(KT):
                    for q in range(QT):
                        c = (k % 2) * S + q * P
                        ins = pe.transpose(ps[:, T[k // 2], c:c + P], nat[:, q, k * P:(k + 1) * P], ident)
                    if k % 2:
                        ins.then_inc(pe_xn, 1)

            def quarter(u0_, plan, j, q, h):
                n = plan.order(j).index((q, h)) + 1
                before = n - 1 if plan.order(j) != QUARTERS and n % 2 == 0 else n - 2
                pe.wait_ge(dve_s, (u0_ + j) * 4 + (before + S0))
                for i in range(2):
                    c0, n = CHUNKS[2 * h + i]
                    dst = ps[:, 2 * h + i, 0:n]
                    qs = slice(q * P, (q + 1) * P)
                    if plan.layer == 0:
                        ins = pe.matmul(dst, q0[:, j % GRP, qs], k0[:, c0:c0 + n], start=True, stop=True)
                    else:
                        ins = unit_mm(pe, dst, [v[:, j, qs] for v in qT_hl],
                                      [v[:, c0:c0 + n] for v in kT_hl], THREE, True, True)
                ins.then_inc(pe_s, 1)

            def queries0(i, bank):
                for j in range(2):
                    ins = pe.matmul(ps[:, bank, j * S:(j + 1) * S], wqk_sb[0:LQ, 2 * i + j, :],
                                    cqT[0:LQ, :], start=True, stop=True)
                ins.then_inc(pe_q0, 1)

            def units(u0_, plan, b, blk_in_b, between=None):
                layer = plan.layer

                def scores(j, q, h):
                    if layer == 0 and j == GRP and (q, h) == (0, 0):
                        pe.wait_ge(dve_q0, (b * BLK0 + blk_in_b) * 4 + 8)
                    quarter(u0_, plan, j, q, h)

                def ring_free(use):
                    kind, n = plan.before(use) or (None, 0)
                    if kind == "T":
                        pe.wait_ge(dve_pT, u0_ * STEPS + (n + 1 + PT0))
                    if kind == "Y":
                        pe.wait_ge(dve_y, u0_ * QT + (n + 1 + Y0))
                    if kind == "Q":
                        pe.wait_ge(dve_q0, (b * BLK0 + blk_in_b) * 4 + (4 + 2 * (n + 1)))

                def queries(i):
                    if i == 0:
                        pe.wait_ge(dma_wqk, (b * BLK0 + blk_in_b) * 16 + 32)
                    ring_free(("Q", i))
                    queries0(i, plan.bank(("Q", i)))

                def transposes(s):
                    j, k = divmod(s, STEPS)
                    if k == 0:
                        pe.wait_ge(act_p, (u0_ + j) * QT + QT)
                    ring_free(("T", s))
                    for i in range(min(2, TT - 2 * k)):
                        t = 2 * k + i
                        n = keys_in(t)
                        for q in range(QT):
                            c = i * S + q * P
                            ins = pe.transpose(ps[0:n, plan.bank(("T", s)), c:c + P],
                                               probs[:, j % 2, q, t * P:t * P + n], ident)
                    ins.then_inc(pe_pT, 1)

                def values(j, k):
                    u = u0_ + j
                    pe.wait_ge(dve_pT, u * STEPS + (k + 1 + PT0))
                    if k == 0:
                        pe.wait_ge(dve_u, u + U0_)
                    dst = ps[:, U, (j % 2) * S:(j % 2 + 1) * S]
                    for i in range(min(2, TT - 2 * k)):
                        t = 2 * k + i
                        n = keys_in(t)
                        right = [v[0:n, (j * STEPS + k) % 3, i * S:(i + 1) * S] for v in pT_hl]
                        first, last = t == 0, t == TT - 1
                        if layer == 0:
                            ins = unit_mm(pe, dst, [v0[0:n, t, :]], right, ((0, 0), (0, 1)), first, last)
                        else:
                            ins = unit_mm(pe, dst, [v[0:n, t, :] for v in v_hl], right, THREE, first, last)
                    ins.then_inc(pe_av, 1)

                def outputs(j, q):
                    u = u0_ + j
                    if q == 0:
                        pe.wait_ge(dve_u, u + (1 + U0_))
                        if layer == 1:
                            pe.wait_ge(pool_wo, (b * KVH + blk_in_b) * GRP + (j + 1))
                    use = ("Y", j * QT + q)
                    ring_free(use)
                    bank = plan.bank(use)
                    qs = slice(q * P, (q + 1) * P)
                    if layer == 0:
                        ins = pe.matmul(ps[:, bank, 0:LKV], u0[:, j % 2, qs],
                                        wvu_sb[:, bass.ds(blk_in_b * (GRP * LKV) + j * LKV, LKV)], start=True, stop=True)
                    else:
                        ins = unit_mm(pe, ps[:, bank, :], [v[:, j % 2, qs] for v in uT_hl],
                                      [v[:, j % 2, :] for v in wo_hl], THREE, True, True)
                    ins.then_inc(pe_y, 1)

                for q, h in plan.first_scores():
                    scores(0, q, h)
                for j, i in plan.others(-1, SCORE_AT):
                    scores(j, *QUARTERS[i])
                if not plan.cont:
                    for s in range(AHEAD):
                        transposes(s)
                for s in range(BLOCK_STEPS):
                    if plan.exists(("T", s + AHEAD)):
                        transposes(s + AHEAD)
                    for j, i in plan.others(s, SCORE_AT):
                        scores(j, *QUARTERS[i])
                    if layer == 0 and plan.more and s in Q0_STEPS:
                        queries(Q0_STEPS[s])
                    for j, q in plan.outs(s, OUT_STEPS):
                        outputs(j, q)
                    if between:
                        between(s)
                    values(*divmod(s, STEPS))
                if between:
                    between(BLOCK_STEPS)
                if not plan.more:
                    for q in range(QT):
                        outputs(GRP - 1, q)

            def queries1(q, pair, blk):
                for k in range(KT):
                    ins = unit_mm(pe, ps[:, q, pair * S:(pair + 1) * S],
                                  [v[:, k, q * P:(q + 1) * P] for v in xnT_hl],
                                  [v[:, pair, k, :] for v in wq_hl], THREE, k == 0, k == KT - 1)
                if pair == 1:
                    ins.then_inc(pe_q, 1)

            def kv_tile(t, blk):
                if 2 <= t < 4:
                    pe.wait_ge(dve_qn, blk * QT + QT)
                if KV_BANKS[t] in KV_BANKS[:t]:
                    last = t - 1 - KV_BANKS[:t][::-1].index(KV_BANKS[t])
                    pe.wait_ge(dve_kn, blk * TT + (last + 1))
                    pe.wait_ge(dve_v, blk * TT + (last + 1))
                n = keys_in(t)
                dst = ps[0:n, KV_BANKS[t], 0:2 * HD].rearrange("p (w d) -> p w d", d=HD)
                for k in range(KT):
                    ins = unit_mm(pe, dst, [v[:, k, t * P:t * P + n] for v in ctx_hl],
                                  [v[:, :, k, :] for v in wkv_hl], THREE, k == 0, k == KT - 1)
                ins.then_inc(pe_kv, 1)

            def attention1(b, g, plan, more):
                blk = b * KVH + g
                u0_ = b * UNITS + g * GRP + H0

                def k_transpose(t):
                    pe.wait_ge(dve_kn, blk * TT + (t + 1))
                    c = t // 4
                    if t % 4 == 0:
                        if c < 2:
                            pe.wait_ge(dve_qT, blk * 2 + 2)
                        else:
                            pe.wait_ge(dve_kT, blk * 4 + (c - 1))
                    n = keys_in(t)
                    ins = pe.transpose(ps[:, T[c % 2], (t % 4) * P:(t % 4) * P + n],
                                       knat[0:n, t % 4, :], ident[0:n, 0:n])
                    ins.then_inc(pe_knat, 1)

                pe.wait_ge(dve_y, u0_ * QT + Y0)
                for t in range(TT):
                    if t >= KV_EARLY:
                        kv_tile(t, blk)
                    if t == Q_AT:
                        pe.wait_ge(dve_qn, blk * QT + QT)
                        for j in range(GRP):
                            for q in range(QT):
                                c = (j % 2) * S + q * P
                                ins = pe.transpose(ps[:, T[j // 2], c:c + P],
                                                   nat[:, q, j * P:(j + 1) * P], ident)
                            if j % 2:
                                ins.then_inc(pe_qT, 1)
                    if t >= K_LAG:
                        k_transpose(t - K_LAG)
                    if t == TT - 1:
                        pe.wait_ge(dve_kT, blk * 4 + 2)
                        quarter(u0_, plan, 0, *FIRST_HALVES[0])
                for t in range(TT - K_LAG, TT):
                    k_transpose(t)
                quarter(u0_, plan, 0, *FIRST_HALVES[1])
                pe.wait_ge(dve_kT, blk * 4 + 4)

                def next_block(s):
                    if s == min(Q1_STEPS):
                        pe.wait_ge(pool_split, blk * SPLITB + (SPLIT0 + SPLITB - 1))
                        pe.wait_ge(dve_s, u0_ * 4 + (GRP * 4 + S0))
                    if s in Q1_STEPS:
                        queries1(*Q1_STEPS[s], blk + 1)
                    if s == BLOCK_STEPS:
                        for t in range(KV_EARLY):
                            kv_tile(t, blk + 1)

                units(u0_, plan, b, g, next_block if more else None)

            def batch(b, more):
                pe.wait_ge(pool_split, 1)
                pe.wait_ge(dve_ctx, b * KT + KT)
                for c, (c0, n) in enumerate(CHUNKS):
                    for k in range(KT):
                        ins = unit_mm(pe, ps[:, c, 0:n], [v[:, k, :] for v in wdkv_hl],
                                      [v[:, k, c0:c0 + n] for v in ctx_hl], THREE, k == 0, k == KT - 1)
                    ins.then_inc(pe_k0, 1)
                transpose_x(b * LN_PER_B)
                pe.wait_ge(act_xnT, b * LN_PER_B * 2 + 2)
                pe.wait_ge(dma_wqd, b * 16 + 16)
                for k in range(KT):
                    ins = pe.matmul(ps[0:LQ, Y, 0:S], wqd_sb[:, k, :], xnT_f[:, k, :], start=(k == 0),
                                    stop=(k == KT - 1))
                ins.then_inc(pe_cq, 1)
                for t in range(TT):
                    if t == 0:
                        pe.wait_ge(dve_k0, b * 4 + 4)
                    if t % 4 == 0 and t >= 8:
                        pe.wait_ge(act_v0, b * 4 + (t // 4 - 1))
                    n = keys_in(t)
                    ins = pe.transpose(ps[0:n, T[t // 4 % 2], (t % 4) * P:(t % 4 + 1) * P],
                                       raw(k0[:, t * P:t * P + n]), ident)
                    if t % 4 == 3 or t == TT - 1:
                        ins.then_inc(pe_v0, 1)
                pe.wait_ge(act_v0, b * 4 + 4)
                wait_alone(pe, (dve_cq, b + 1))
                pe.wait_ge(dma_wqk, b * (BLK0 * 16) + 16)
                for i in range(2):
                    queries0(i, RING[i])
                pe.wait_ge(dma_const, 48)
                wait_alone(pe, (dve_q0, b * (BLK0 * 4) + 4))
                layer0_blocks(pe, lambda k, plan: units(b * UNITS + k * GRP, plan, b, k))

                transpose_x(b * LN_PER_B + 1)
                pe.wait_ge(act_xnT, b * LN_PER_B * 2 + 4)
                pe.wait_ge(dma_ffn, b * 64 + 64)
                for q in range(QT):
                    qs = slice(q * P, (q + 1) * P)
                    for k in range(KT):
                        ins = pe.matmul(ps[:, LOW[q], 0:AG], xnT_f[:, k, qs], ag_sb[:, k, :],
                                        start=(k == 0), stop=(k == KT - 1))
                    ins.then_inc(pe_low, 1)
                for q in range(QT):
                    qs = slice(q * P, (q + 1) * P)
                    for k in range(KT):
                        pe.matmul(ps[:, RES[q], :], xnT_f[:, k, qs], base_sb[:, k, :], start=(k == 0),
                                  stop=False)
                    pe.matmul(ps[:, RES[q], :], ones[0:1, :], baseb_sb[0:1, :], start=False, stop=False)
                for q in range(QT):
                    pe.wait_ge(dve_lw, b * QT + (q + 1))
                    pe.transpose(ps[:, TRN[q], 0:P], lw[:, q, :], ident).then_inc(pe_lw, 1)
                for q in range(QT):
                    pe.wait_ge(act_lw, b * QT + (q + 1))
                    pe.matmul(ps[:, RES[q], :], lwT[:, q, :], lorab_sb, start=False,
                              stop=True).then_inc(pe_res, 1)

                transpose_x(b * LN_PER_B + 2)
                wait_alone(pe, (dve_xnT, b * 2 + 2))
                pe.wait_ge(pool_split, b * (KVH * SPLITB) + SPLIT0)
                for q, pair in Q1_STEPS.values():
                    queries1(q, pair, b * KVH)
                for t in range(KV_EARLY):
                    kv_tile(t, b * KVH)
                layer1_blocks(pe, lambda g, plan, more: attention1(b, g, plan, more))

            batches(pe, batch)

            def x_transposes(t):
                pe.wait_ge(dve_xnat, t + 1)
                if t >= 2:
                    pe.wait_ge(dve_xlo, t - 1)
                    pe.wait_ge(act_xg, t - 1)
                for k in range(KT):
                    ins = pe.transpose(ps[:, T[t % 2], k * P:(k + 1) * P],
                                       xnat[t % 2][:, k * P:(k + 1) * P], ident)
                ins.then_inc(pe_mx, 1)

            x_transposes(0)
            for t in range(TOK):
                if t + 1 < TOK:
                    x_transposes(t + 1)
                pe.wait_ge(act_xg, t + 1)
                if t == 0:
                    pe.wait_ge(dma_gate, 32)
                for k in range(KT):
                    ins = pe.matmul(ps[:, Y, t * E1:(t + 1) * E1], xnT_g[t % 2][:, k, :], gate_sb[:, k, :],
                                    start=(k == 0), stop=(k == KT - 1))
                ins.then_inc(pe_lg, 1)
            pe.wait_ge(dve_xlo, TOK)
            pe.wait_ge(act_lg, 1)
            base = B * KVH * SPLITB + SPLIT0

            def expert(e, buf):
                pe.wait_ge(pool_split, base + 1 + e)
                for c in range(2):
                    for it in range(2):
                        n = 2 * c + it
                        pe.wait_ge(dve_z, e * 4 + (n + 1 - 2 + Z0))
                        for which in range(2):
                            w = [gu_w(buf, part, which) for part in range(2)]
                            for k in range(KT):
                                ins = unit_mm(pe, ps[:, 2 * (n % 2) + which, :],
                                              [v[:, k, it * P:(it + 1) * P] for v in w],
                                              [v[:, k, c * 512:(c + 1) * 512] for v in xnT_all], THREE,
                                              k == 0, k == KT - 1)
                        ins.then_inc(pe_gu, 1)
                for t in range(TOK):
                    pe.wait_ge(dve_zl, e * 4 + ((2 if t < TOK // 2 else 4) + Z0))
                    pe.wait_ge(dve_dn, e * TOK + (t + 1 - 4 + DN0))
                    for it in range(2):
                        ins = unit_mm(pe, ps[:, 4 + t % 4, :], [v[:, it, t * P:(t + 1) * P] for v in z_hl],
                                      [dn_w(buf, part)[:, it, :] for part in range(2)], THREE, it == 0,
                                      it == 1)
                    ins.then_inc(pe_dn, 1)

            with pe.Fori(0, E1 // 2) as i:
                expert(i * 2, 0)
                expert(i * 2 + 1, 1)
            expert(E1, 0)

        @block.scalar
        def _(act):
            act.preload_act_table(ACT.Exp)

            def copy(dst, src, **kw):
                return act.activation(dst, src, ACT.Copy, **kw)

            def xnT_copies(ln, layer1):
                for i in range(2):
                    act.wait_ge(pe_xn, ln * 2 + (i + 1))
                    dst = (xnT_hl[0] if layer1 else xnT_f)[:, 2 * i:2 * i + 2, :]
                    copy(dst, ps[:, T[i], :].rearrange("p (k s) -> p k s", s=S)).then_inc(act_xnT, 1)

            def queries0(i, bank):
                act.activation(q0[:, 2 * i:2 * i + 2, :], ps[:, bank, :].rearrange("p (k s) -> p k s", s=S),
                               ACT.Copy, scale=float(LKV) ** -0.5).then_inc(act_q0, 1)

            def units(u0_, plan, b, blk_in_b, between=None):
                layer = plan.layer

                def exps(j, q):
                    u = u0_ + j
                    act.wait_ge(dve_max, u * QT + (q + 1))
                    act.activation(probs[:, j % 2, q, 0:NK], probs[:, j % 2, q, 0:NK], ACT.Exp,
                                   bias=negmax[:, j % 2, q:q + 1],
                                   accum_out=rowsum[:, j % GRP, q:q + 1]).then_inc(act_p, 1)

                def highs(j, k):
                    u = u0_ + j
                    act.wait_ge(pe_pT, u * STEPS + (k + 1 + PP0))
                    s = j * STEPS + k
                    act.wait_ge(pe_av, u0_ * STEPS + (max(s - 2, 0) + AV0))
                    n, c = step_cols(k)
                    copy(pT_hl[0][0:n, s % 3, c], ps[0:n, plan.bank(("T", s)), c]).then_inc(act_pT, 1)

                def head(j):
                    u = u0_ + j
                    act.wait_ge(pe_av, (u + 1) * STEPS + AV0)
                    src = ps[:, U, (j % 2) * S:(j % 2 + 1) * S]
                    dst = u0 if layer == 0 else uT_hl[0]
                    copy(dst[:, j % 2, :], src).then_inc(act_u, 1)

                if not plan.cont:
                    for q in range(QT):
                        exps(0, q)
                for s in range(BLOCK_STEPS):
                    highs(*divmod(s, STEPS))
                    for j in plan.heads_done(s):
                        head(j)
                    for j, q in plan.others(s, EXP_AT):
                        exps(j, q)
                    if layer == 0 and plan.more and s - 1 in Q0_STEPS:
                        i = Q0_STEPS[s - 1]
                        act.wait_ge(pe_q0, (b * BLK0 + blk_in_b) * 2 + (2 + i + 1 + Q0))
                        queries0(i, plan.bank(("Q", i)))
                    if between:
                        between(s)
                if not plan.more:
                    head(GRP - 1)

            def squares1(q, blk):
                act.wait_ge(pe_q, blk * QT + (q + 1))
                for j in range(GRP):
                    n = q * GRP + j
                    if n >= 2:
                        act.wait_ge(act_qss, blk * (QT * GRP) + (n - 1))
                    act.activation(junk[:, n % 2, :], ps[:, q, j * P:(j + 1) * P], ACT.Square,
                                   accum_out=qss[:, n:n + 1]).then_inc(act_qss, 1)

            def ctx_high(b, k):
                act.wait_ge(dma_ctx[k], b * 16 + 16)
                copy(ctx_hl[0][:, k, 0:NK], ctx_raw[k]).then_inc(act_ctx, 1)

            def attention1(b, g, plan, more):
                blk = b * KVH + g
                act.wait_ge(act_qss, blk * (QT * GRP) + QT * GRP)

                def kv(t):
                    n = keys_in(t)
                    act.wait_ge(pe_kv, blk * TT + (t + 1 + KV0))
                    if t >= 2:
                        act.wait_ge(act_kss, blk * TT + (t - 1))
                    act.activation(junk[0:n, t % 2, :], ps[0:n, KV_BANKS[t], 0:P], ACT.Square,
                                   accum_out=ssq[0:n, t:t + 1]).then_inc(act_kss, 1)
                    copy(v_hl[0][0:n, t, :], ps[0:n, KV_BANKS[t], P:2 * P]).then_inc(act_v, 1)

                def kT(c):
                    act.wait_ge(pe_knat, blk * TT + min(4 * c + 4, TT))
                    n = min(512, NK - 512 * c)
                    copy(kT_hl[0][:, 512 * c:512 * c + n], ps[:, T[c % 2], 0:n],
                         scale=norm_w[:, 1:2]).then_inc(act_kT, 1)

                for t in range(TT):
                    kv(t)
                    if t == Q_AT:
                        for i in range(2):
                            act.wait_ge(pe_qT, blk * 2 + (i + 1))
                            copy(qT_hl[0][:, 2 * i:2 * i + 2, :],
                                 ps[:, T[i], :].rearrange("p (k s) -> p k s", s=S),
                                 scale=norm_w[:, 0:1]).then_inc(act_qT, 1)
                    if t >= K_LAG + 3 and (t - K_LAG - 3) % 4 == 0:
                        kT((t - K_LAG - 3) // 4)
                for c in range(2, 4):
                    kT(c)
                act.wait_ge(act_kss, blk * TT + TT)

                def next_block(s):
                    if s in SQUARE_STEPS:
                        squares1(SQUARE_STEPS[s], blk + 1)

                units(b * UNITS + g * GRP + H0, plan, b, g, next_block if more else None)

            def batch(b, more):
                for c, (c0, n) in enumerate(CHUNKS):
                    act.wait_ge(pe_k0, b * 4 + (c + 1))
                    n = min(n, NK - c0)
                    copy(k0[:, c0:c0 + n], ps[:, c, 0:n]).then_inc(act_k0, 1)
                xnT_copies(b * LN_PER_B, False)
                for c in range(4):
                    act.wait_ge(pe_v0, b * 4 + (c + 1))
                    if c < 3:
                        copy(v0[:, 4 * c:4 * c + 4, :],
                             ps[:, T[c % 2], :].rearrange("p (t d) -> p t d", d=P)).then_inc(act_v0, 1)
                    else:
                        copy(v0[0:LAST, TT - 1, :], ps[0:LAST, T[c % 2], 0:P]).then_inc(act_v0, 1)
                for i in range(2):
                    act.wait_ge(pe_q0, b * (BLK0 * 2) + (i + 1 + Q0))
                    queries0(i, RING[i])
                layer0_blocks(act, lambda k, plan: units(b * UNITS + k * GRP, plan, b, k))
                act.wait_ge(dma_const, 48)
                xnT_copies(b * LN_PER_B + 1, False)
                act.wait_ge(dve_gate, b + 1)
                act.activation(g_e, g_a, ACT.Exp).then_inc(act_ge, 1)
                for q in range(QT):
                    act.wait_ge(pe_lw, b * QT + (q + 1))
                    copy(lwT[:, q, :], ps[:, TRN[q], 0:P]).then_inc(act_lw, 1)
                xnT_copies(b * LN_PER_B + 2, True)
                for q in range(QT):
                    squares1(q, b * KVH)
                layer1_blocks(act, lambda g, plan, more_g: attention1(b, g, plan, more_g))
                act.wait_ge(dve_y, (b + 1) * (UNITS * QT) + Y0)
                act.dma_start(x_mid[b].rearrange("t p d -> p t d"), xb).then_inc(dma_x_out, 16)
                if more:
                    for k in range(KT):
                        ctx_high(b + 1, k)

            for k in range(KT):
                ctx_high(0, k)
            batches(act, batch)

            for t in range(TOK):
                act.wait_ge(pe_mx, t + 1)
                src = ps[:, T[t % 2], :].rearrange("p (k s) -> p k s", s=P)
                copy(xnT_all[0][:, :, t * P:(t + 1) * P], src).then_inc(act_xhi, 1)
                if t >= 2:
                    act.wait_ge(pe_lg, t - 1)
                copy(xnT_g[t % 2], src).then_inc(act_xg, 1)
            act.wait_ge(pe_lg, TOK)
            act.activation(sc, ps[:, Y, 0:TOK * E1].rearrange("p (t e) -> p t e", e=E1),
                           ACT.Sigmoid).then_inc(act_lg, 1)

            act.preload_act_table(ACT.Silu)

            act.sem_inc(act_z, Z0)
            act.wait_ge(dve_cw, 1)

            def expert(e):
                def silu(n):
                    act.wait_ge(pe_gu, e * 4 + (n + 1))
                    act.wait_ge(dve_z, e * 4 + (n + 1 - 2 + Z0))
                    act.activation(sil[:, n % 2, :], ps[:, 2 * (n % 2), :], ACT.Silu).then_inc(act_sil, 1)

                def high(n):
                    act.wait_ge(dve_z, e * 4 + (n + 1 + Z0))
                    c, it = n // 2, n % 2
                    copy(z_hl[0][:, it, c * 512:(c + 1) * 512], zf[:, n % 2, :]).then_inc(act_z, 1)

                silu(0)
                for n in range(1, 4):
                    silu(n)
                    high(n - 1)
                high(3)

            with act.Fori(0, E1 + 1) as e:
                expert(e)

        @block.vector
        def _(dve):
            dve.sem_inc(dve_s, S0)
            dve.sem_inc(dve_pT, PT0)
            dve.sem_inc(dve_u, U0_)
            dve.sem_inc(dve_z, Z0)
            dve.sem_inc(dve_y, Y0)
            dve.sem_inc(dve_zl, Z0)
            dve.wait_ge(pool_const, CONSTS)
            dve.sem_inc(dve_dn, DN0)

            def low(dst, src, hi):
                return dve.tensor_tensor(dst, src, raw(hi), ALU.subtract)

            def layernorm(ln):
                for q in range(QT):
                    dve.bn_stats(stats[:, q, :], xb[:, q, :]).then_inc(dve_stat, 1)
                for q in range(QT):
                    wait_alone(dve, (dve_stat, ln * QT + (q + 1)))
                    dve.bn_aggr(mv[:, q, :], stats[:, q, :]).then_inc(dve_var, 1)
                dve.wait_ge(pool_rstd, ln + 1)
                for q in range(QT):
                    dve.tensor_scalar(nat[:, q, :], xb[:, q, :], mv[:, q, 0:1], rstd[:, q:q + 1],
                                      ALU.subtract, ALU.mult).then_inc(dve_xn, 1)

            def row_max(u0_, plan, j, q, h):
                u = u0_ + j
                n = u * 4 + (plan.order(j).index((q, h)) + 1)
                dve.wait_ge(pe_s, n)
                if q == 0 and h == 0:
                    dve.wait_ge(pe_pT, u * STEPS + (PP0 - STEPS))
                p = j % 2
                k0_, w = HALVES[h]
                dst = probs[:, p, q, k0_:k0_ + w]
                if h == 1:
                    dve.wait_ge(dve_s, u * 4 + (plan.order(j).index((q, 0)) + 1 + S0))
                wait_alone(dve)
                first = NEG if h == 0 else mx_a[:, p, q:q + 1]
                acc = (mx_a if h == 0 else mx)[:, p, q:q + 1]
                if plan.layer == 0:
                    add = strided(zero, 0, (0, w))
                else:
                    add = mask_sb[:, q, k0_:k0_ + w]
                dve.tensor_tensor_reduce(dst, s_half(h, w), add, 1.0, first, ALU.add, ALU.max,
                                         acc).then_inc(dve_s, 1)
                if h == 1:
                    dve.wait_ge(dve_s, n + S0)
                    dve.tensor_scalar(negmax[:, p, q:q + 1], mx[:, p, q:q + 1], -1.0, None,
                                      ALU.mult).then_inc(dve_max, 1)

            def queries0(i, bank):
                for row in (LKV, 3 * LKV):
                    cols = q0[row:row + LKV, 2 * i:2 * i + 2, :]
                    dve.scalar_tensor_tensor(
                        out=cols, in0=ps[row:row + LKV, bank, :].rearrange("p (k s) -> p k s", s=S),
                        scalar=float(LKV) ** -0.5, in1=raw(cols), op0=ALU.mult,
                        op1=ALU.subtract).then_inc(dve_q0, 1)

            def units(u0_, plan, b, kk, between=None):
                layer = plan.layer

                def maxima(j, q, h):
                    row_max(u0_, plan, j, q, h)

                def lows(j, k):
                    u = u0_ + j
                    s = j * STEPS + k
                    n, c = step_cols(k)
                    dve.wait_ge(act_pT, u * STEPS + (k + 1))
                    low(pT_hl[1][0:n, s % 3, c], ps[0:n, plan.bank(("T", s)), c],
                        pT_hl[0][0:n, s % 3, c]).then_inc(dve_pT, 1)

                def head(j):
                    u = u0_ + j
                    p = j % 2
                    dve.wait_ge(act_u, u + 1)
                    dve.reciprocal(rinv[:, p, :], rowsum[:, j % GRP, :]).then_inc(dve_rinv, 1)
                    if layer == 0:
                        dve.sem_inc(dve_u, 1)
                    else:
                        low(uT_hl[1][:, p, :], ps[:, U, p * S:(p + 1) * S],
                            uT_hl[0][:, p, :]).then_inc(dve_u, 1)

                def add_out(j, q):
                    u = u0_ + j
                    dve.wait_ge(pe_y, u * QT + (q + 1))
                    if q == 0:
                        dve.wait_ge(dve_rinv, u + 1)
                    bank = plan.bank(("Y", j * QT + q))
                    if layer == 0:
                        cols = xb[:, q, bass.ds(kk * (GRP * LKV) + j * LKV, LKV)]
                        src = ps[:, bank, 0:LKV]
                    else:
                        cols, src = xb[:, q, :], ps[:, bank, :]
                    dve.scalar_tensor_tensor(out=cols, in0=src, scalar=rinv[:, j % 2, q:q + 1], in1=cols,
                                             op0=ALU.mult, op1=ALU.add).then_inc(dve_y, 1)

                for q, h in plan.first_scores():
                    maxima(0, q, h)
                for j, i in plan.others(-1, MAX_AT):
                    maxima(j, *QUARTERS[i])
                for s in range(BLOCK_STEPS):
                    lows(*divmod(s, STEPS))
                    for j in plan.heads_done(s):
                        head(j)
                    for j, i in plan.others(s, MAX_AT):
                        maxima(j, *QUARTERS[i])
                    if layer == 0 and plan.more and s - 1 in Q0_STEPS:
                        i = Q0_STEPS[s - 1]
                        dve.wait_ge(act_q0, (b * BLK0 + kk) * 2 + (2 + i + 1))
                        queries0(i, plan.bank(("Q", i)))
                    for j, q in plan.outs(s, ADD_STEPS):
                        add_out(j, q)
                    if between:
                        between(s)
                if not plan.more:
                    head(GRP - 1)
                    if between:
                        between(BLOCK_STEPS)
                    for q in range(QT):
                        add_out(GRP - 1, q)

            def q_norm(blk):
                dve.wait_ge(pool_rq, blk + 1)
                for q in range(QT):
                    dve.tensor_tensor(nat[:, q, :].rearrange("p (h d) -> p h d", d=HD),
                                      ps[:, q, :].rearrange("p (h d) -> p h d", d=HD),
                                      strided(rq, q * GRP, (1, GRP), (0, HD)),
                                      ALU.mult).then_inc(dve_qn, 1)

            def ctx_low(b, k):
                dve.wait_ge(act_ctx, b * KT + (k + 1))
                low(ctx_hl[1][:, k, 0:NK], ctx_raw[k], ctx_hl[0][:, k, 0:NK]).then_inc(dve_ctx, 1)

            def attention1(b, g, plan, more):
                blk = b * KVH + g
                u0_ = b * UNITS + g * GRP + H0

                def v_low(t):
                    n = keys_in(t)
                    dve.wait_ge(act_v, blk * TT + (t + 1))
                    low(v_hl[1][0:n, t, :], ps[0:n, KV_BANKS[t], P:2 * P],
                        v_hl[0][0:n, t, :]).then_inc(dve_v, 1)

                def k_norm(t):
                    n = keys_in(t)
                    dve.wait_ge(pool_rk, blk * TT + (t + 1))
                    if t >= 4:
                        dve.wait_ge(pe_knat, blk * TT + (t - 3))
                    dve.tensor_scalar(knat[0:n, t % 4, :], ps[0:n, KV_BANKS[t], 0:P], rk[0:n, t:t + 1], None,
                                      ALU.mult).then_inc(dve_kn, 1)

                def kT(c):
                    dve.wait_ge(act_kT, blk * 4 + (c + 1))
                    n = min(512, NK - 512 * c)
                    cols = slice(512 * c, 512 * c + n)
                    dve.scalar_tensor_tensor(out=kT_hl[1][:, cols], in0=ps[:, T[c % 2], 0:n],
                                             scalar=norm_w[:, 1:2], in1=raw(kT_hl[0][:, cols]),
                                             op0=ALU.mult, op1=ALU.subtract).then_inc(dve_kT, 1)

                for t in range(TT):
                    v_low(t)
                    if t:
                        k_norm(t - 1)
                    if t == Q_AT:
                        for i in range(2):
                            dve.wait_ge(act_qT, blk * 2 + (i + 1))
                            cols = qT_hl[0][:, 2 * i:2 * i + 2, :]
                            dve.scalar_tensor_tensor(
                                out=qT_hl[1][:, 2 * i:2 * i + 2, :],
                                in0=ps[:, T[i], :].rearrange("p (k s) -> p k s", s=S),
                                scalar=norm_w[:, 0:1], in1=raw(cols), op0=ALU.mult,
                                op1=ALU.subtract).then_inc(dve_qT, 1)
                    if t >= K_LAG + 3 and (t - K_LAG - 3) % 4 == 0:
                        kT((t - K_LAG - 3) // 4)
                k_norm(TT - 1)
                row_max(u0_, plan, 0, *FIRST_HALVES[0])
                for c in range(2, 4):
                    kT(c)
                row_max(u0_, plan, 0, *FIRST_HALVES[1])

                def next_block(s):
                    if s == BLOCK_STEPS:
                        q_norm(blk + 1)

                units(u0_, plan, b, g, next_block if more else None)

            link_n = [0]
            LINKS = 9

            def link(b, ins):
                link_n[0] += 1
                ins.then_inc(dve_link, 1)
                dve.wait_ge(dve_link, b * LINKS + link_n[0])

            def ranks(b, score, rank, work, n, e):
                per_j = strided(score, 0, (e, n), (0, e), (1, e))
                per_e = strided(score, 0, (e, n), (1, e), (0, e))
                before = strided(tri[:, 0, :], 0, (0, n), (E1, e), (1, e))
                gt, eq = [strided(w, 0, (e * e, n), (e, e), (1, e)) for w in work]
                dve.tensor_tensor(gt, per_j, per_e, ALU.is_gt).then_inc(dve_cmp, 1)
                link(b, dve.tensor_tensor(eq, per_j, per_e, ALU.is_equal))
                link(b, dve.tensor_tensor(eq, eq, before, ALU.mult))
                link(b, dve.tensor_tensor(gt, gt, eq, ALU.add))
                link(b, dve.tensor_reduce(rank, gt, AX_X, ALU.add))

            def batch(b, more):
                dve.wait_ge(dma_x, b * 16 + 16)
                layernorm(b * LN_PER_B)
                for c, (c0, n) in enumerate(CHUNKS):
                    n = min(n, NK - c0)
                    dve.wait_ge(act_k0, b * 4 + (c + 1))
                    cols = k0[P // 2:, c0:c0 + n]
                    low(cols, ps[P // 2:, c, 0:n], cols).then_inc(dve_k0, 1)
                dve.wait_ge(pe_cq, b + 1)
                dve.tensor_copy(cqT[0:LQ, :], ps[0:LQ, Y, 0:S]).then_inc(dve_cq, 1)
                for i in range(2):
                    dve.wait_ge(act_q0, b * (BLK0 * 2) + (i + 1))
                    queries0(i, RING[i])
                layer0_blocks(dve, lambda k, plan: units(b * UNITS + k * GRP, plan, b, k))
                dve.wait_ge(dma_const, 48)
                dve.wait_ge(dve_y, b * (UNITS * QT) + (H0 * QT + Y0))
                layernorm(b * LN_PER_B + 1)
                link_n[0] = 0
                dve.wait_ge(pe_low, b * QT + QT)
                link(b, dve.tensor_copy(gate, ps[:, LOW[0]:LOW[0] + 2, E0 * R0:AG]))
                link(b, dve.tensor_reduce(g_m, gate, AX_X, ALU.max))
                dve.tensor_tensor(g_a, gate, strided(g_m, 0, (1, QT), (0, E0)),
                                  ALU.subtract).then_inc(dve_gate, 1)
                ranks(b, gate, g_rank, cmp0, QT, E0)
                dve.wait_ge(act_ge, b + 1)
                link(b, dve.scalar_tensor_tensor(out=g_a, in0=g_rank, scalar=2.0, in1=g_e, op0=ALU.is_lt,
                                                 op1=ALU.mult))
                link(b, dve.tensor_reduce(g_sum, g_a, AX_X, ALU.add))
                link(b, dve.reciprocal(g_m, g_sum))
                assert link_n[0] == LINKS
                dve.scalar_tensor_tensor(out=g_rank, in0=g_a, scalar=2.0,
                                         in1=strided(g_m, 0, (1, QT), (0, E0)), op0=ALU.mult,
                                         op1=ALU.mult).then_inc(dve_w, 1)
                dve.wait_ge(dve_w, b + 1)
                for q in range(QT):
                    dve.tensor_tensor(strided(lw[:, q, :], 0, (R0, E0), (1, R0)),
                                      ps[:, LOW[q], 0:P].rearrange("p (e r) -> p e r", r=R0),
                                      strided(g_rank[:, q, :], 0, (1, E0), (0, R0)),
                                      ALU.mult).then_inc(dve_lw, 1)
                for q in range(QT):
                    dve.wait_ge(pe_res, b * QT + (q + 1))
                    dve.tensor_tensor(xb[:, q, :], xb[:, q, :], ps[:, RES[q], :], ALU.add).then_inc(dve_ffn, 1)
                dve.wait_ge(dve_ffn, b * QT + QT)
                layernorm(b * LN_PER_B + 2)
                for i in range(2):
                    dve.wait_ge(act_xnT, b * (LN_PER_B * 2) + (4 + i + 1))
                    low(xnT_hl[1][:, 2 * i:2 * i + 2, :], ps[:, T[i], :].rearrange("p (k s) -> p k s", s=S),
                        xnT_hl[0][:, 2 * i:2 * i + 2, :]).then_inc(dve_xnT, 1)
                q_norm(b * KVH)
                layer1_blocks(dve, lambda g, plan, more_g: attention1(b, g, plan, more_g))
                if more:
                    for k in range(KT):
                        ctx_low(b + 1, k)

            for k in range(KT):
                ctx_low(0, k)
            batches(dve, batch)

            for t in range(TOK):
                dve.wait_ge(dma_xall[t // QT], 16)
                dve.bn_stats(stats[:, t, :], x_all[:, t, :]).then_inc(dve_stat, 1)
            for t in range(TOK):
                dve.wait_ge(dve_stat, B * LN_PER_B * QT + (t + 1))
                dve.bn_aggr(mv[:, t, :], stats[:, t, :]).then_inc(dve_var, 1)
            dve.wait_ge(pool_rstd, B * LN_PER_B + 1)

            def x_low(t):
                dve.wait_ge(act_xg, t + 1)
                cols = xnT_all[0][:, :, t * P:(t + 1) * P]
                low(xnT_all[1][:, :, t * P:(t + 1) * P],
                    ps[:, T[t % 2], :].rearrange("p (k s) -> p k s", s=P), cols).then_inc(dve_xlo, 1)

            for t in range(TOK):
                if t >= 2:
                    dve.wait_ge(pe_mx, t - 1)
                dve.tensor_scalar(xnat[t % 2], x_all[:, t, :], mv[:, t, 0:1], rstd[:, t:t + 1],
                                  ALU.subtract, ALU.mult).then_inc(dve_xnat, 1)
                if t:
                    x_low(t - 1)
            x_low(TOK - 1)
            link_n[0] = 0
            b = B
            dve.wait_ge(act_lg, 1)
            dve.wait_ge(dma_gate, 32)
            dve.memset(cw, 1.0).then_inc(dve_cmp, 1)
            link(b, dve.tensor_tensor(sc, sc, strided(bias_sb, 0, (0, TOK), (1, E1)), ALU.add))
            ranks(b, sc, rank, cmp1, TOK, E1)
            link(b, dve.scalar_tensor_tensor(out=rank, in0=rank, scalar=float(TOPK), in1=sc, op0=ALU.is_lt,
                                             op1=ALU.mult))
            link(b, dve.tensor_reduce(wsum, rank, AX_X, ALU.add))
            link(b, dve.tensor_scalar(wsum, wsum, 1e-20, None, ALU.add))
            link(b, dve.reciprocal(wsum, wsum))
            dve.tensor_tensor(cw[:, :, 0:E1], rank, strided(wsum, 0, (1, TOK), (0, E1)),
                              ALU.mult).then_inc(dve_cw, 1)
            dve.wait_ge(dve_cw, 1)

            def expert(e):
                def product(n):
                    dve.wait_ge(act_sil, e * 4 + (n + 1))
                    dve.wait_ge(dve_zl, e * 4 + (n + 1 - 2 + Z0))
                    dve.wait_ge(act_z, e * 4 + (n + 1 - 2 + Z0))
                    dve.tensor_tensor(zf[:, n % 2, :], sil[:, n % 2, :], ps[:, 2 * (n % 2) + 1, :],
                                      ALU.mult).then_inc(dve_z, 1)

                def z_low(n):
                    dve.wait_ge(act_z, e * 4 + (n + 1 + Z0))
                    c, it = n // 2, n % 2
                    cols = slice(c * 512, (c + 1) * 512)
                    low(z_hl[1][:, it, cols], zf[:, n % 2, :], z_hl[0][:, it, cols]).then_inc(dve_zl, 1)

                product(0)
                for n in range(1, 4):
                    product(n)
                    z_low(n - 1)
                z_low(3)
                for t in range(TOK):
                    dve.wait_ge(pe_dn, e * TOK + (t + 1))
                    dve.scalar_tensor_tensor(out=x_all[:, t, :], in0=ps[:, 4 + t % 4, :],
                                             scalar=cw[:, t, bass.ds(e, 1)], in1=x_all[:, t, :],
                                             op0=ALU.mult, op1=ALU.add).then_inc(dve_dn, 1)

            with dve.Fori(0, E1 + 1) as e:
                expert(e)


def kernel(**inputs):
    import numpy as np
    import concourse.bacc as bacc
    from concourse.bass_utils import run_bass_kernel_spmd as run

    a = {k: np.asarray(v) for k, v in inputs.items()}

    def rows(w, n):
        r = w.reshape(w.shape[:-2] + (w.shape[-2] // P, P, n))
        return np.swapaxes(r, -3, -2)

    def ahead(w):
        return np.concatenate([w, w[:1]], axis=0)

    wqk = a["L0_xattn_W_qk"].reshape(LQ, BLK0, GRP, 1, LKV)
    wqk = np.broadcast_to(wqk, (LQ, BLK0, GRP, 4, LKV)).reshape(LQ, BLK0, GRP, P).transpose(1, 0, 2, 3)
    wdkv = np.broadcast_to(a["L0_xattn_Wkv_d"][:, None, :], (D, 4, LKV)).reshape(D, P)
    wvu = np.zeros((4, LKV, H0 * LKV), np.float32)
    wvu[0] = wvu[2] = a["L0_xattn_Wv_u"]
    ag = np.concatenate([a["L0_ffn_lora_A"].reshape(E0 * R0, D), a["L0_ffn_gate_w"]], axis=0).T
    wq = a["L1_xattn_Wq"].reshape(KVH, 2, 2 * HD, D).transpose(0, 1, 3, 2)
    wo = a["L1_xattn_Wo"].T.reshape(KVH, 2, 2, HD, D).transpose(0, 1, 3, 2, 4)
    wg = np.concatenate([a["L1_ffn_Wg"], a["L1_ffn_Sg"][None]], axis=0).transpose(0, 2, 1)
    wu = np.concatenate([a["L1_ffn_Wu"], a["L1_ffn_Su"][None]], axis=0).transpose(0, 2, 1)
    wd = np.concatenate([a["L1_ffn_Wd"], a["L1_ffn_Sd"][None]], axis=0).transpose(0, 2, 1)
    laid = {
        "x": a["x"].reshape(B, QT, P, D),
        "ctx_t": a["ctx_4096"].transpose(0, 2, 1).reshape(B, KT, P, NK),
        "mask": a["mask_1x1xSxS2_ff0"].reshape(QT, P, NK),
        "wqd": rows(a["L0_xattn_Wq_d"], LQ),
        "wqk": wqk,
        "wdkv": rows(wdkv, P),
        "wvu": wvu.reshape(P, H0 * LKV),
        "ag_t": rows(ag, AG),
        "base_t": rows(a["L0_ffn_base_w"].T, D),
        "base_b": a["L0_ffn_base_b"].reshape(1, D),
        "lora_b": a["L0_ffn_lora_B"].transpose(0, 2, 1).reshape(E0 * R0, D),
        "wk": ahead(rows(a["L1_xattn_Wk"].reshape(KVH, HD, D).transpose(0, 2, 1), HD)),
        "wv": ahead(rows(a["L1_xattn_Wv"].reshape(KVH, HD, D).transpose(0, 2, 1), HD)),
        "wq": ahead(rows(wq, 2 * HD).reshape(KVH, 2, P, KT * 2 * HD)),
        "wo": wo.reshape(KVH, 2, P, 2 * D),
        "norms": np.stack([a["L1_xattn_q_norm_w"], a["L1_xattn_k_norm_w"]], axis=1),
        "gate_t": rows(a["L1_ffn_gate_w"].T, E1),
        "gate_bias": np.broadcast_to(a["L1_ffn_bias"], (P, E1)),
        "wg": rows(wg, INNER).reshape(E1 + 1, P, KT * INNER),
        "wu": rows(wu, INNER).reshape(E1 + 1, P, KT * INNER),
        "wd": rows(wd, D).reshape(E1 + 1, P, 2 * D),
    }
    nc = bacc.Bacc("TRN2", target_bir_lowering=False, num_devices=1)
    arrays, args = {}, {}
    for name, v in laid.items():
        v = np.ascontiguousarray(v)
        arrays[f"in_{name}"] = v
        args[name] = nc.dram_tensor(f"in_{name}", v.shape, mybir.dt.from_np(v.dtype),
                                    kind="ExternalInput").ap()
    args["out"] = nc.dram_tensor("out_x", (B, QT, P, D), F32, kind="ExternalOutput").ap()
    args["x_mid"] = nc.dram_tensor("x_mid", (B, QT, P, D), F32, kind="Internal").ap()
    xattn_ffn_kernel(nc, **args)
    r = run(nc, [arrays], core_ids=[0])
    return np.asarray(r.results[0]["out_x"]).reshape(B, S, D)
```
